# Optimizing a Trainium2 kernel written in Bass

```python
import numpy as np
import jax
import jax.numpy as jnp

def _softmax(x, axis=-1):
    return jax.nn.softmax(x, axis=axis)

def _gelu(x):
    return jax.nn.gelu(x, approximate=True)

def _silu(x):
    return jax.nn.silu(x)

def _sigmoid(x):
    return jax.nn.sigmoid(x)

def _layernorm(x, axis=-1, eps=1e-05):
    m = jnp.mean(x, axis=axis, keepdims=True)
    v = jnp.var(x, axis=axis, keepdims=True)
    return (x - m) / jnp.sqrt(v + eps)

def _scatter_add(tgt, idx, src, axis=0):
    return tgt.at[idx].add(src)

def _segment_sum(src, seg, n):
    return jax.ops.segment_sum(src, seg, n)
kernel_name = 'mk_flamingo_gated_d1_seqx_r4_c39f7c'

def setup_inputs(seed: int=0):
    np.random.seed(seed)
    _w = jnp.asarray

    def _rec_inputs():
        import jax
        import jax.numpy as jnp
        _rk = jax.random.key(seed)
        x = 0.002226 + 0.9996 * jax.random.normal(jax.random.fold_in(_rk, 1), (16, 112, 256), jnp.float32)
        _lenS = 112 - jax.random.randint(jax.random.fold_in(_rk, 7), (16,), 0, max(1, 112 // 4) + 1, jnp.int32)
        _lenS2 = 375 - jax.random.randint(jax.random.fold_in(_rk, 8), (16,), 0, max(1, 375 // 4) + 1, jnp.int32)
        _ctx_1024P = jax.random.normal(jax.random.fold_in(_rk, 11), (16, 16, 256), jnp.float32)
        _ctx_1024c = jax.random.dirichlet(jax.random.fold_in(_rk, 511), 0.3 * jnp.ones((16,), jnp.float32), (16, 375))
        _ctx_1024t = jnp.einsum('bsk,bkd->bsd', _ctx_1024c, _ctx_1024P)
        _ctx_1024t = _ctx_1024t * jax.lax.rsqrt(jnp.mean(jnp.square(_ctx_1024t)) + 1e-12) * 0.953939
        ctx_1024 = -0.000125008 + 0.999885 * (_ctx_1024t + 0.3 * jax.random.normal(jax.random.fold_in(_rk, 611), (16, 375, 256), jnp.float32))
        _g = jax.random.normal(jax.random.fold_in(_rk, 9001), (2, 1), jnp.float32)
        _g = jnp.sign(_g) * jnp.maximum(jnp.abs(_g), 1.0) + (_g == 0) * 1.0
        g_xattn = _g[0]
        g_ffn = _g[1]
        return (x, ctx_1024, g_xattn, g_ffn)
    x, ctx_1024, g_xattn, g_ffn = _rec_inputs()

    def _L0_xattn_setup():
        import jax, jax.numpy as jnp
        import numpy as np
        DIM = 256
        HEADS = 16
        DIM_HEAD = 64
        INNER = HEADS * DIM_HEAD
        EPS = 1e-05

        def _layernorm(x, w, b):
            m = jnp.mean(x, axis=-1, keepdims=True)
            v = jnp.mean(jnp.square(x - m), axis=-1, keepdims=True)
            return (x - m) * jax.lax.rsqrt(v + EPS) * w + b
        key = jax.random.key(seed)
        ks = jax.random.split(key, 9)
        B, N, L = (8, 1024, 64)
        x = jax.random.normal(ks[0], (B, N, DIM), dtype=jnp.float32)
        latents = jax.random.normal(ks[1], (B, L, DIM), dtype=jnp.float32)
        s = 1.0 / np.sqrt(DIM)
        Wq = jax.random.normal(ks[2], (DIM, INNER), dtype=jnp.float32) * s
        Wkv = jax.random.normal(ks[3], (DIM, 2 * INNER), dtype=jnp.float32) * s
        Wo = jax.random.normal(ks[4], (INNER, DIM), dtype=jnp.float32) * (1.0 / np.sqrt(INNER))
        ln1_w = jnp.ones((DIM,), jnp.float32)
        ln1_b = jnp.zeros((DIM,), jnp.float32)
        ln2_w = jnp.ones((DIM,), jnp.float32)
        ln2_b = jnp.zeros((DIM,), jnp.float32)
        return {'x': x, 'latents': latents, 'Wq': Wq, 'Wkv': Wkv, 'Wo': Wo, 'ln1_w': ln1_w, 'ln1_b': ln1_b, 'ln2_w': ln2_w, 'ln2_b': ln2_b}
    _L0_xattn_all = _L0_xattn_setup()
    _L0_xattn_in = {k: v for k, v in _L0_xattn_all.items() if k in ('Wq', 'Wkv', 'Wo', 'ln1_w', 'ln1_b', 'ln2_w', 'ln2_b')}
    del _L0_xattn_all

    def _L0_ffn_setup():
        import jax, jax.numpy as jnp
        import numpy as np
        B, S, H, I, E, K = (4, 512, 256, 688, 4, 2)
        key = jax.random.key(seed)
        ks = jax.random.split(key, 8)
        inv_h = 1.0 / np.sqrt(H)
        inv_i = 1.0 / np.sqrt(I)
        return {'x': jax.random.normal(ks[0], (B, S, H), jnp.float32), 'gate_w': jax.random.normal(ks[1], (E, H), jnp.float32) * inv_h, 'eg': jax.random.normal(ks[2], (E, I, H), jnp.float32) * inv_h, 'eu': jax.random.normal(ks[3], (E, I, H), jnp.float32) * inv_h, 'ed': jax.random.normal(ks[4], (E, H, I), jnp.float32) * inv_i, 'sg': jax.random.normal(ks[5], (I, H), jnp.float32) * inv_h, 'su': jax.random.normal(ks[6], (I, H), jnp.float32) * inv_h, 'sd': jax.random.normal(ks[7], (H, I), jnp.float32) * inv_i}
    _L0_ffn_all = _L0_ffn_setup()
    _L0_ffn_in = {k: v for k, v in _L0_ffn_all.items() if k in ('gate_w', 'eg', 'eu', 'ed', 'sg', 'su', 'sd')}
    del _L0_ffn_all
    return {'x': x, 'ctx_1024': ctx_1024, 'g_xattn': g_xattn, 'g_ffn': g_ffn, 'L0_xattn_Wq': _L0_xattn_in['Wq'], 'L0_xattn_Wkv': _L0_xattn_in['Wkv'], 'L0_xattn_Wo': _L0_xattn_in['Wo'], 'L0_xattn_ln1_w': _L0_xattn_in['ln1_w'], 'L0_xattn_ln1_b': _L0_xattn_in['ln1_b'], 'L0_xattn_ln2_w': _L0_xattn_in['ln2_w'], 'L0_xattn_ln2_b': _L0_xattn_in['ln2_b'], 'L0_ffn_gate_w': _L0_ffn_in['gate_w'], 'L0_ffn_eg': _L0_ffn_in['eg'], 'L0_ffn_eu': _L0_ffn_in['eu'], 'L0_ffn_ed': _L0_ffn_in['ed'], 'L0_ffn_sg': _L0_ffn_in['sg'], 'L0_ffn_su': _L0_ffn_in['su'], 'L0_ffn_sd': _L0_ffn_in['sd']}

def reference(x, ctx_1024, g_xattn, g_ffn, L0_xattn_Wq, L0_xattn_Wkv, L0_xattn_Wo, L0_xattn_ln1_w, L0_xattn_ln1_b, L0_xattn_ln2_w, L0_xattn_ln2_b, L0_ffn_gate_w, L0_ffn_eg, L0_ffn_eu, L0_ffn_ed, L0_ffn_sg, L0_ffn_su, L0_ffn_sd):
    import jax
    import jax.numpy as jnp

    def _L0_xattn_ref(x, latents, Wq, Wkv, Wo, ln1_w, ln1_b, ln2_w, ln2_b):
        import jax, jax.numpy as jnp
        import numpy as np
        DIM = 256
        HEADS = 16
        DIM_HEAD = 64
        INNER = HEADS * DIM_HEAD
        EPS = 1e-05

        def _layernorm(x, w, b):
            m = jnp.mean(x, axis=-1, keepdims=True)
            v = jnp.mean(jnp.square(x - m), axis=-1, keepdims=True)
            return (x - m) * jax.lax.rsqrt(v + EPS) * w + b
        B, L, _ = latents.shape
        xn = _layernorm(x, ln1_w, ln1_b)
        ln = _layernorm(latents, ln2_w, ln2_b)
        q = ln @ Wq
        kv_input = jnp.concatenate([xn, ln], axis=-2)
        kv = kv_input @ Wkv
        k, v = jnp.split(kv, 2, axis=-1)

        def heads(t):
            b, s, _ = t.shape
            return t.reshape(b, s, HEADS, DIM_HEAD).transpose(0, 2, 1, 3)
        q, k, v = (heads(q), heads(k), heads(v))
        scale = 1.0 / np.sqrt(np.sqrt(DIM_HEAD))
        logits = jnp.einsum('bhld,bhsd->bhls', q * scale, k * scale)
        w = jax.nn.softmax(logits.astype(jnp.float32), axis=-1).astype(logits.dtype)
        out = jnp.einsum('bhls,bhsd->bhld', w, v)
        out = out.transpose(0, 2, 1, 3).reshape(B, L, INNER)
        return out @ Wo

    def _L0_ffn_ref(x, gate_w, eg, eu, ed, sg, su, sd):
        import jax, jax.numpy as jnp
        import numpy as np
        B, S, H, I, E, K = (4, 512, 256, 688, 4, 2)
        xf = x.reshape(-1, x.shape[-1])
        scores = jax.nn.softmax(xf @ gate_w.T, axis=-1)
        topk_w, topk_idx = jax.lax.top_k(scores, K)
        topk_w = topk_w / (topk_w.sum(axis=-1, keepdims=True) + 1e-20)
        comb = jnp.sum(jax.nn.one_hot(topk_idx, E, dtype=x.dtype) * topk_w[..., None], axis=1)
        g = jax.nn.silu(jnp.einsum('nh,eih->eni', xf, eg))
        u = jnp.einsum('nh,eih->eni', xf, eu)
        y_exp = jnp.einsum('eni,ehi->enh', g * u, ed)
        y = jnp.einsum('enh,ne->nh', y_exp, comb)
        y = y + jax.nn.silu(xf @ sg.T) * (xf @ su.T) @ sd.T
        return y.reshape(x.shape)
    x = x + jnp.tanh(g_xattn[0]) * _L0_xattn_ref(ctx_1024, _layernorm(x, axis=-1), L0_xattn_Wq, L0_xattn_Wkv, L0_xattn_Wo, L0_xattn_ln1_w, L0_xattn_ln1_b, L0_xattn_ln2_w, L0_xattn_ln2_b)
    x = x + jnp.tanh(g_ffn[0]) * _L0_ffn_ref(_layernorm(x, axis=-1), L0_ffn_gate_w, L0_ffn_eg, L0_ffn_eu, L0_ffn_ed, L0_ffn_sg, L0_ffn_su, L0_ffn_sd)
    return x

_drawn_inputs = setup_inputs


def setup_inputs(seed=0):
    import zlib

    import numpy as np

    out = dict(_drawn_inputs(seed))
    spreads = {'L0_xattn_ln1_w': (1.0, 0.2),
     'L0_xattn_ln1_b': (0.0, 0.1),
     'L0_xattn_ln2_w': (1.0, 0.2),
     'L0_xattn_ln2_b': (0.0, 0.1)}
    factors = {}
    for name, (base, spread) in spreads.items():
        noise = np.random.default_rng([zlib.crc32(name.encode()), seed]).standard_normal(out[name].shape)
        drawn = base * np.exp(spread * noise) if base else spread * noise
        out[name] = jnp.asarray(drawn.astype(out[name].dtype))
    for name, factor in factors.items():
        out[name] = (out[name] * factor).astype(out[name].dtype)
    return out
```

```python
from contextlib import ExitStack

import concourse.bass as bass
from concourse import mybir

ALU = mybir.AluOpType
ACT = mybir.ActivationFunctionType
AX = mybir.AxisListType
F32 = mybir.dt.float32
F32R = mybir.dt.float32r

EPS = 1e-5
P = 128
DH = 64
KT = 4
CT = 3
PAIRS = 8
GB = 4


def flamingo_block(nc, x, ctx_in, g_xattn, g_ffn, Wq, Wkv, Wo, ln_wb,
                   gate_wT, gateT, upT, downT, out):
    B, L, D = x.shape
    S = ctx_in.shape[1]
    INNER = Wq.shape[1]
    E1, _, I = gateT.shape
    E = E1 - 1
    C = D // P
    SK = S + L
    KW = (SK + KT - 1) // KT * KT
    KR = KW // KT
    SR = S // CT
    H = INNER // DH
    assert H == 2 * PAIRS and S % CT == 0 and KW - SK == 1 and C == 2
    N = B * L
    GT = GB * L
    G = B // GB
    MS = [116] * 4 + [112] * 2
    MO = [sum(MS[:m]) for m in range(6)]
    M6 = len(MS)
    assert sum(MS) == I
    GUW = 2 * C * I
    FW = GUW + M6 * D
    SPLIT = lambda t: t.bitcast(F32)

    with ExitStack() as life:
        def sem(name):
            return life.enter_context(nc.semaphore(name))

        def sb(stack, name, shape, dt=F32):
            return stack.enter_context(nc.sbuf_tensor(name, shape, dt))

        x1 = sb(life, "x1", [L, B, D])
        raw = sb(life, "raw", [P, FW])
        ident = sb(life, "ident", [P, P])
        gates = sb(life, "gates", [P, 2])
        tgate = sb(life, "tgate", [P, 2])
        neghalf = sb(life, "neghalf", [P, B])
        ffn_st = sb(life, "ffn_st", [L, B, 6])
        ffn_mv = sb(life, "ffn_mv", [L, B, 2])
        ffn_ve = sb(life, "ffn_ve", [L, B])
        ffn_rstd = sb(life, "ffn_rstd", [L, B])

        one = ExitStack()
        wkv_h = sb(one, "wkv_h", [P, C, 2 * INNER], F32R)
        wkv_l = sb(one, "wkv_l", [P, C, 2 * INNER], F32R)
        wo_h = sb(one, "wo_h", [P, PAIRS, D], F32R)
        wo_l = sb(one, "wo_l", [P, PAIRS, D], F32R)
        wq = sb(one, "wq", [P, C, INNER])
        lnw = sb(one, "lnw", [P, 4, C])
        ctx_raw = sb(one, "ctx_raw", [SR, CT, D])
        rows = sb(one, "rows", [SR, CT + 1, D])
        st = sb(one, "st", [SR, CT + 1, 6])
        mv = sb(one, "mv", [SR, CT + 1, 2])
        ve = sb(one, "ve", [SR, CT + 1])
        rstd = sb(one, "rstd", [SR, CT + 1])
        lst = sb(one, "lst", [L, 6])
        lmv = sb(one, "lmv", [L, 2])
        lve = sb(one, "lve", [L, 1])
        lrstd = sb(one, "lrstd", [L, 1])
        val = sb(one, "val", [P, C, KW])
        kv_h = sb(one, "kv_h", [P, C, KW], F32R)
        kv_l = sb(one, "kv_l", [P, C, KW], F32R)
        xq = sb(one, "xq", [P, C, L])
        k_h = sb(one, "k_h", [P, PAIRS, KW], F32R)
        k_l = sb(one, "k_l", [P, PAIRS, KW], F32R)
        q_h = sb(one, "q_h", [P, PAIRS, L], F32R)
        q_l = sb(one, "q_l", [P, PAIRS, L], F32R)
        v = sb(one, "v", [KR, KT, INNER])
        nmax = sb(one, "nmax", [L, H])
        rsum = sb(one, "rsum", [L, H])
        rinv = sb(one, "rinv", [L, H])
        prob = sb(one, "prob", [L, 4, KW])
        probT = sb(one, "probT", [KR, 4, KT, L])
        o_h = sb(one, "o_h", [P, PAIRS, L], F32R)
        o_l = sb(one, "o_l", [P, PAIRS, L], F32R)
        one.close()

        two = ExitStack()
        w_h = [sb(two, f"w_h{i}", [P, FW], F32R) for i in range(2)]
        w_l = [sb(two, f"w_l{i}", [P, FW], F32R) for i in range(2)]
        xn_h = sb(two, "xn_h", [P, C, N], F32R)
        xn_l = sb(two, "xn_l", [P, C, N], F32R)
        accT = sb(two, "accT", [P, C, N])
        xrow = [sb(two, f"xrow{i}", [L, D]) for i in range(2)]
        xnT = [sb(two, f"xnT{i}", [P, C, L]) for i in range(2)]
        gw = sb(two, "gw", [P, C, E])
        lg = sb(two, "lg", [L, B, E])
        lmax = sb(two, "lmax", [L, B])
        ex = sb(two, "ex", [L, B, E])
        esum = sb(two, "esum", [L, B])
        sc = sb(two, "sc", [L, B, E])
        beat = sb(two, "beat", [L, E, B, E])
        rank = sb(two, "rank", [L, B, E])
        wsel = sb(two, "wsel", [L, B, E])
        wsum = sb(two, "wsum", [L, B])
        comb = sb(two, "comb", [L, E, B])
        combT = sb(two, "combT", [E * B, L])
        cb = [sb(two, f"cb{i}", [P, N]) for i in range(2)]
        sl = sb(two, "sl", [P, 2, GT])
        hf = sb(two, "hf", [P, 2, GT])
        h_h = sb(two, "h_h", [P, M6, GT], F32R)
        h_l = sb(two, "h_l", [P, M6, GT], F32R)
        ytmp = sb(two, "ytmp", [P, C, GT])
        two.close()
        comb_dram = nc.dram_tensor("comb_dram", (E * B, L), F32, kind="Internal").ap()

        bank = [life.enter_context(nc.psum_tensor(f"bank{i}", [P, 512], F32)) for i in range(8)]
        bS = bank[0:2]
        bT = bank[2:4]
        bK, bV, bO, bM = bank[4:8]
        gb, ub, yb = bank[0:2], bank[4:6], [bank[6], bank[2]]

        x_in, ctx_loaded, small_in, wq_in, out_done = map(sem, (
            "x_in", "ctx_loaded", "small_in", "wq_in", "out_done"))
        wk_in, wv_in, wo_in = map(sem, ("wk_in", "wv_in", "wo_in"))
        wk_hi, wk_lo, wv_hi, wv_lo, wo_hi, wo_lo = map(sem, (
            "wk_hi", "wk_lo", "wv_hi", "wv_lo", "wo_hi", "wo_lo"))
        ident0, const_set, tanh_done = map(sem, ("ident0", "const_set", "tanh_done"))
        stats, aggr, var_eps, rstd_done, lat_done = map(sem, (
            "stats", "aggr", "var_eps", "rstd_done", "lat_done"))
        lstats, laggr, lvar_eps, lrstd_done, rows_done = map(sem, (
            "lstats", "laggr", "lvar_eps", "lrstd_done", "rows_done"))
        kvt_done, val_done, kv_hi_done, kv_lo_done, xq_done = map(sem, (
            "kvt_done", "val_done", "kv_hi_done", "kv_lo_done", "xq_done"))
        kproj, k_hi_done, k_lo_done, vproj, v_out, qproj, q_hi_done, q_lo_done = map(sem, (
            "kproj", "k_hi_done", "k_lo_done", "vproj", "v_out", "qproj", "q_hi_done", "q_lo_done"))
        scored, maxed, exped, inverted, normed, turned, turned_out = map(sem, (
            "scored", "maxed", "exped", "inverted", "normed", "turned", "turned_out"))
        pv_done, o_hi_done, o_lo_done, wo_done, x1_done, fstats, faggr = map(sem, (
            "pv_done", "o_hi_done", "o_lo_done", "wo_done", "x1_done", "fstats", "faggr"))
        fve_done, frstd, xrow_done, xt_done, xn_hi_done, xn_copied, xn_lo_done, gated = map(sem, (
            "fve_done", "frstd", "xrow_done", "xt_done", "xn_hi_done", "xn_copied", "xn_lo_done", "gated"))
        route, route_exp, comb_t, comb_c, comb_out = map(sem, (
            "route", "route_exp", "comb_t", "comb_c", "comb_out"))
        cb_in = [sem(f"cb_in{i}") for i in range(2)]
        ffw_in, ffw_hi, ffw_piece, ffw_lo, gw_in = map(sem, (
            "ffw_in", "ffw_hi", "ffw_piece", "ffw_lo", "gw_in"))
        gate_mm, up_mm, silu_done, h_mul, h_hi_done, h_lo_done, down_mm, y_out, acc_done = map(sem, (
            "gate_mm", "up_mm", "silu_done", "h_mul", "h_hi_done", "h_lo_done", "down_mm", "y_out",
            "acc_done"))
        yt_done, fin, waited = map(sem, ("yt_done", "fin", "waited"))

        S0 = 1
        T0 = 3
        C0 = 2
        V0 = 2
        O0 = 1
        X0 = 1
        W0 = 1
        R0 = 2
        G0 = 1
        H0 = 2
        D0 = 1
        Y0 = 1
        A0 = 1

        ROUTED = 12

        def plain(eng):
            eng.sem_inc(waited, 1)

        block = life.enter_context(nc.Block())

        @block.sync
        def _(sp):
            def load_ctx(t):
                if not isinstance(t, int):
                    sp.wait_ge(lat_done, t)
                elif t > 0:
                    sp.wait_ge(lat_done, t)
                sp.dma_start(ctx_raw[:, :, :],
                             ctx_in[bass.ds(t, 1), :, :].rearrange("a (c p) d -> p (a c) d", p=SR)
                             ).then_inc(ctx_loaded, 16)

            load_ctx(0)
            sp.dma_start(x1[:, :, :], x.rearrange("b l d -> l b d")).then_inc(x_in, 16)
            sp.dma_start(lnw[:, :, :], ln_wb).then_inc(small_in, 16)
            sp.dma_start(gates[:, 0:1], g_xattn.rearrange("(a n) -> a n", a=1).broadcast_to((P, 1))
                         ).then_inc(small_in, 16)
            sp.dma_start(gates[:, 1:2], g_ffn.rearrange("(a n) -> a n", a=1).broadcast_to((P, 1))
                         ).then_inc(small_in, 16)
            for c in range(C):
                sp.dma_start(raw[:, c * INNER:(c + 1) * INNER],
                             Wkv[c * P:(c + 1) * P, 0:INNER]).then_inc(wk_in, 16)
            sp.dma_start(wq[:, :, :], Wq.rearrange("(c p) n -> p c n", p=P)).then_inc(wq_in, 16)
            for c in range(C):
                sp.dma_start(raw[:, (C + c) * INNER:(C + c + 1) * INNER],
                             Wkv[c * P:(c + 1) * P, INNER:2 * INNER]).then_inc(wv_in, 16)
            load_ctx(1)
            sp.wait_ge(wk_lo, C)
            sp.dma_start(raw[:, 0:PAIRS * D].rearrange("p (j d) -> p j d", j=PAIRS),
                         Wo.rearrange("(j p) d -> p j d", p=P)).then_inc(wo_in, 16)
            with sp.Fori(2, B) as t:
                load_ctx(t)

            def load_expert(k):
                gate = gateT[k, :, :].rearrange("(c p) i -> p c i", p=P)
                up = upT[k, :, :].rearrange("(c p) i -> p c i", p=P)
                for n, w in enumerate((gate, up)):
                    sp.dma_start(raw[:, n * C * I:(n + 1) * C * I].rearrange("p (c i) -> p c i", c=C),
                                 w).then_inc(ffw_in, 16)
                for m0, m1 in ((0, 4), (4, M6)):
                    sp.dma_start(
                        raw[0:MS[m0], GUW + m0 * D:GUW + m1 * D].rearrange("p (m d) -> p m d", d=D),
                        downT[k, MO[m0]:MO[m0] + (m1 - m0) * MS[m0], :].rearrange(
                            "(m p) d -> p m d", p=MS[m0])).then_inc(ffw_in, 16)

            def load_comb(k):
                sp.dma_start(cb[k % 2][:, :],
                             comb_dram[(k - 1) * B:k * B, :].rearrange("b l -> (b l)")
                             .partition_broadcast(P)).then_inc(cb_in[k % 2], 16)

            sp.wait_ge(wv_lo, C)
            sp.wait_ge(wo_lo, 1)
            load_expert(0)
            sp.wait_ge(x1_done, X0 + B)
            sp.dma_start(gw[:, :, :], gate_wT.rearrange("(c p) e -> p c e", p=P)
                         ).then_inc(gw_in, 16)
            sp.wait_ge(ffw_lo, 1)
            load_expert(1)
            sp.wait_ge(comb_c, 1)
            sp.dma_start(comb_dram, combT[:, :]).then_inc(comb_out, 16)
            sp.wait_ge(comb_out, 16)
            load_comb(1)
            load_comb(2)
            for k in range(2, E1):
                sp.wait_ge(ffw_lo, k)
                load_expert(k)
                if k >= 3:
                    sp.wait_ge(y_out, Y0 + C * G * (k - 1))
                    load_comb(k)
            QB = B // 4
            for q in range(4):
                sp.wait_ge(fin, QB * (q + 1))
                sp.dma_start(out[q * QB:(q + 1) * QB, :, :].rearrange("b l d -> l b d"),
                             x1[:, q * QB:(q + 1) * QB, :]).then_inc(out_done, 16)
            sp.wait_ge(out_done, 64)

        @block.tensor
        def _(pe):
            def three(out_ap, w_hi, w_lo, m_hi, m_lo, start, stop):
                pe.matmul(out_ap, w_hi, m_hi, start=start, stop=False)
                pe.matmul(out_ap, w_hi, m_lo, start=False, stop=False)
                return pe.matmul(out_ap, w_lo, m_hi, start=False, stop=stop)

            def turn_rows(t, c, bank_free):
                pe.wait_ge(rows_done, t + 1)
                for s, at_least in bank_free:
                    pe.wait_ge(s, at_least)
                for r in range(CT + 1):
                    n = SR if r < CT else L
                    mm = pe.transpose(bM[:, r * SR:r * SR + n], rows[0:n, r, c * P:(c + 1) * P],
                                      ident[0:n, 0:n])
                mm.then_inc(kvt_done, 1)

            def project_q(t, half, bank_free):
                pe.wait_ge(xq_done, t + 1)
                for s, at_least in bank_free:
                    pe.wait_ge(s, at_least)
                for i in range(4):
                    j = 4 * half + i
                    for c in range(C):
                        mm = pe.matmul(bM[:, i * L:(i + 1) * L], wq[:, c, j * P:(j + 1) * P],
                                       xq[:, c, :], start=(c == 0), stop=(c == C - 1))
                mm.then_inc(qproj, 1)

            def project_k(t, j):
                if j == 0:
                    pe.wait_ge(kv_lo_done, t + 1)
                    if not (isinstance(t, int) and t == 0):
                        pe.wait_ge(v_out, PAIRS * t)
                else:
                    pe.wait_ge(k_lo_done, PAIRS * t + j)
                for c in range(C):
                    mm = three(bK[:, 0:KW], wkv_h[:, c, j * P:(j + 1) * P],
                               wkv_l[:, c, j * P:(j + 1) * P], kv_h[:, c, :], kv_l[:, c, :],
                               c == 0, c == C - 1)
                mm.then_inc(kproj, 1)

            def project_v(t, i, half):
                last = (i, half) == (PAIRS // 2 - 1, 1)
                to = bK if last else bV
                if last:
                    pe.wait_ge(k_lo_done, PAIRS * (t + 1))
                elif i or half:
                    pe.wait_ge(v_out, PAIRS * t + 2 * i + half)
                for n in range(2):
                    for c in range(C):
                        s = 2 * half + n
                        cols = slice(INNER + 2 * P * i, INNER + 2 * P * (i + 1))
                        keys = slice(s * KR, (s + 1) * KR)
                        mm = three(to[0:KR, n * 2 * P:(n + 1) * 2 * P], kv_h[:, c, keys],
                                   kv_l[:, c, keys], wkv_h[:, c, cols], wkv_l[:, c, cols],
                                   c == 0, c == C - 1)
                mm.then_inc(vproj, 1)

            def scores(b, j):
                pe.wait_ge(k_lo_done, PAIRS * b + j + 1)
                pe.wait_ge(q_lo_done, 2 * b + j // 4 + 1)
                for u in range(2):
                    pe.wait_ge(exped, H * b + 2 * j + u)
                    half = slice(DH * u, DH * (u + 1))
                    three(bS[u][0:L, 0:KW], q_h[half, j, :], q_l[half, j, :],
                          k_h[half, j, :], k_l[half, j, :], True, True).then_inc(scored, 1)

            def turn(b, j):
                for u in range(2):
                    n = H * b + 2 * j + u
                    pe.wait_ge(normed, n + 1)
                    pe.wait_ge(turned_out, n + 1)
                    for s in range(KT):
                        mm = pe.transpose(bT[u][0:KR, s * L:(s + 1) * L],
                                          prob[:, (2 * j + u) % 4, s * KR:(s + 1) * KR],
                                          ident[0:L, 0:L])
                    mm.then_inc(turned, 1)

            def weigh(b, j):
                pe.wait_ge(turned_out, C0 + H * b + 2 * j + 2)
                if j % 2 == 0:
                    pe.wait_ge(v_out, PAIRS * b + j + 2)
                if j % 4 == 0:
                    pe.wait_ge(o_lo_done, O0 + 2 * b + j // 4)
                for s in range(KT):
                    for u in range(2):
                        mm = pe.matmul(bO[DH * u:DH * (u + 1), (j % 4) * L:(j % 4 + 1) * L],
                                       v[:, s, P * j + DH * u:P * j + DH * (u + 1)],
                                       probT[:, (2 * j + u) % 4, s, :],
                                       start=(s == 0), stop=(s == KT - 1))
                mm.then_inc(pv_done, 1)

            def project_out(b, bank_free):
                pe.wait_ge(o_lo_done, O0 + 2 * b + 2)
                for s, at_least in bank_free:
                    pe.wait_ge(s, at_least)
                for j in range(PAIRS):
                    mm = three(bM[0:L, 0:D], o_h[:, j, :], o_l[:, j, :], wo_h[:, j, :],
                               wo_l[:, j, :], j == 0, j == PAIRS - 1)
                mm.then_inc(wo_done, 1)

            def batch(b, next1, next2):
                for j in range(PAIRS):
                    if j > 0:
                        scores(b, j)
                        turn(b, j - 1)
                    if next1:
                        project_k(b + 1, j)
                        if j >= 2:
                            project_v(b + 1, (j - 2) // 2, j % 2)
                    if j > 0:
                        weigh(b, j - 1)
                    if next1 and j == 4:
                        project_q(b + 1, 0, [(x1_done, X0 + b)])
                    if next2 and j == 5:
                        turn_rows(b + 2, 0, [(q_lo_done, 2 * b + 3)])
                    if next2 and j == 6:
                        turn_rows(b + 2, 1, [(val_done, 2 * b + 5)])
                if next1:
                    project_q(b + 1, 1, [(val_done, 2 * b + 6)] if next2
                              else [(q_lo_done, 2 * b + 3)])
                turn(b, PAIRS - 1)
                if next1:
                    project_v(b + 1, 3, 0)
                    project_v(b + 1, 3, 1)
                weigh(b, PAIRS - 1)
                if next1:
                    scores(b + 1, 0)
                project_out(b, [(q_lo_done, 2 * b + 4)] if next1 else [(x1_done, X0 + b)])

            pe.wait_ge(const_set, 4)
            turn_rows(0, 0, [])
            turn_rows(0, 1, [(val_done, 1)])
            pe.wait_ge(wq_in, 16)
            project_q(0, 0, [(val_done, 2)])
            pe.wait_ge(wk_lo, C)
            for j in range(PAIRS):
                project_k(0, j)
                if j == 0:
                    project_q(0, 1, [(q_lo_done, 1)])
                if j == 1:
                    scores(0, 0)
                if j == 2:
                    turn_rows(1, 0, [(q_lo_done, 2)])
                if j == 3:
                    turn_rows(1, 1, [(val_done, 3)])
            pe.wait_ge(wv_lo, C)
            for i in range(PAIRS // 2):
                project_v(0, i, 0)
                project_v(0, i, 1)
            pe.wait_ge(wo_lo, 1)
            with pe.Fori(0, B - 2) as b:
                batch(b, True, True)
            batch(B - 2, True, False)
            batch(B - 1, False, False)

            def turn_ffn(b, u):
                pe.wait_ge(xrow_done, b + 1)
                pe.wait_ge(xn_lo_done, b + 1)
                for c in range(C):
                    mm = pe.transpose(bT[u][:, c * L:(c + 1) * L], xrow[u][:, c * P:(c + 1) * P],
                                      ident[0:L, 0:L])
                mm.then_inc(xt_done, 1)

            def gate_scores(b, u):
                pe.wait_ge(xn_copied, b + 1)
                for c in range(C):
                    mm = pe.matmul(bM[0:L, bass.ds(b * E, E)], xnT[u][:, c, :], gw[:, c, :],
                                   start=(c == 0), stop=(c == C - 1))
                mm.then_inc(gated, 1)

            pe.wait_ge(gw_in, 16)
            with pe.Fori(0, B // 2) as i:
                turn_ffn(2 * i, 0)
                turn_ffn(2 * i + 1, 1)
                gate_scores(2 * i, 0)
                gate_scores(2 * i + 1, 1)

            def hidden(k, wt, g, m):
                n = (k * G + g) * M6 + m
                pe.wait_ge(h_mul, n + 1)
                for part, to, done in ((0, gb, gate_mm), (1, ub, up_mm)):
                    for c in range(C):
                        cols = slice((C * part + c) * I + MO[m], (C * part + c) * I + MO[m] + MS[m])
                        tok = bass.ds(g * GT, GT)
                        mm = three(to[m % 2][0:MS[m], 0:GT], w_h[wt][:, cols], w_l[wt][:, cols],
                                   xn_h[:, c, tok], xn_l[:, c, tok], c == 0, c == C - 1)
                    mm.then_inc(done, 1)

            def down(k, wt, g, m):
                n = (k * G + g) * M6 + m
                pe.wait_ge(h_lo_done, H0 + n + 1)
                if m == 0:
                    pe.wait_ge(y_out, Y0 + C * (k * G + g))
                for c in range(C):
                    cols = slice(GUW + m * D + c * P, GUW + m * D + (c + 1) * P)
                    mm = three(yb[c][:, 0:GT], w_h[wt][0:MS[m], cols], w_l[wt][0:MS[m], cols],
                               h_h[0:MS[m], m, :], h_l[0:MS[m], m, :], m == 0, m == M6 - 1)
                mm.then_inc(down_mm, 1)

            def expert(k, wt):
                pe.wait_ge(ffw_lo, k + 1)
                plain(pe)
                with pe.Fori(0, G) as g:
                    hidden(k, wt, g, 0)
                    hidden(k, wt, g, 1)
                    for m in range(2, M6):
                        if m < M6 - 1:
                            down(k, wt, g, m - 2)
                        hidden(k, wt, g, m)
                    for m in range(M6 - 3, M6):
                        down(k, wt, g, m)

            pe.wait_ge(xn_lo_done, R0 + B)
            expert(0, 0)
            pe.wait_ge(route, ROUTED)
            pe.transpose(bM[0:E * B, 0:L], comb[:, :, :].rearrange("l e b -> l (e b)"),
                         ident[0:L, 0:L]).then_inc(comb_t, 1)
            with pe.Fori(0, E // 2) as i:
                expert(2 * i + 1, 1)
                expert(2 * i + 2, 0)

            pe.wait_ge(acc_done, A0 + C * G * E)
            for b in range(B):
                u = b % 2
                if b >= 2:
                    pe.wait_ge(fin, b - 1)
                for c in range(C):
                    mm = pe.transpose(bT[u][0:L, c * P:(c + 1) * P],
                                      accT[:, c, b * L:(b + 1) * L], ident[:, :])
                mm.then_inc(yt_done, 1)

        @block.scalar
        def _(act):
            def split_w(dst, src, loaded, at_least, done):
                act.wait_ge(loaded, at_least)
                act.activation(dst, src, ACT.Copy).then_inc(done, 1)

            def values_in(t, c):
                act.wait_ge(kvt_done, 2 * t + c + 1)
                if not (isinstance(t, int) and t == 0):
                    act.wait_ge(kv_hi_done, t)
                    act.wait_ge(kv_lo_done, t)
                    act.wait_ge(xq_done, t)
                act.activation(val[:, c, 0:S], bM[:, 0:S], ACT.Identity,
                               bias=lnw[:, 1, c:c + 1], scale=lnw[:, 0, c:c + 1])
                act.activation(val[:, c, S:SK], bM[:, S:SK], ACT.Identity,
                               bias=lnw[:, 3, c:c + 1], scale=lnw[:, 2, c:c + 1]
                               ).then_inc(val_done, 1)

            def keys_hi(t, j):
                act.wait_ge(kproj, PAIRS * t + j + 1)
                act.activation(k_h[:, j, :], bK[:, 0:KW], ACT.Copy).then_inc(k_hi_done, 1)

            def values_out(t, i, half):
                act.wait_ge(vproj, PAIRS * t + 2 * i + half + 1)
                if not (isinstance(t, int) and t == 0):
                    act.wait_ge(pv_done, V0 + PAIRS * (t - 1) + 2 * i + 2)
                src = bK if (i, half) == (PAIRS // 2 - 1, 1) else bV
                act.activation(v[:, 2 * half:2 * half + 2, 2 * P * i:2 * P * (i + 1)],
                               src[0:KR, :].rearrange("p (s n) -> p s n", s=2), ACT.Copy
                               ).then_inc(v_out, 1)

            def queries_hi(t, half):
                act.wait_ge(qproj, 2 * t + half + 1)
                act.activation(q_h[:, 4 * half:4 * half + 4, :],
                               bM[:, 0:4 * L].rearrange("p (j l) -> p j l", j=4), ACT.Copy,
                               scale=DH ** -0.5).then_inc(q_hi_done, 1)

            def exps(b, j):
                for u in range(2):
                    h = 2 * j + u
                    act.wait_ge(maxed, H * b + h + 1)
                    act.wait_ge(turned, H * b + h)
                    act.activation(prob[:, h % 4, 0:SK], bS[u][0:L, 0:SK], ACT.Exp,
                                   bias=nmax[:, h:h + 1], accum_out=rsum[:, h:h + 1]
                                   ).then_inc(exped, 1)

            def heads_hi(b, half):
                act.wait_ge(pv_done, V0 + PAIRS * b + 4 * half + 4)
                act.wait_ge(wo_done, W0 + b)
                act.activation(o_h[:, 4 * half:4 * half + 4, :],
                               bO[:, 0:4 * L].rearrange("p (j l) -> p j l", j=4), ACT.Copy
                               ).then_inc(o_hi_done, 1)

            def batch(b, next1, next2):
                for j in range(PAIRS):
                    if j > 0:
                        exps(b, j)
                    if next1:
                        keys_hi(b + 1, j)
                        if j >= 2:
                            values_out(b + 1, (j - 2) // 2, j % 2)
                        if j == 4:
                            queries_hi(b + 1, 0)
                    if j == 4:
                        heads_hi(b, 0)
                    if next2 and j >= 5 and j < 7:
                        values_in(b + 2, j - 5)
                if next1:
                    queries_hi(b + 1, 1)
                heads_hi(b, 1)
                if next1:
                    values_out(b + 1, 3, 0)
                    values_out(b + 1, 3, 1)
                    exps(b + 1, 0)

            act.wait_ge(small_in, 48)
            act.wait_ge(const_set, 4)
            act.activation(tgate[:, :], gates[:, :], ACT.Tanh).then_inc(tanh_done, 1)
            for c in range(C):
                split_w(wkv_h[:, c, 0:INNER], raw[:, c * INNER:(c + 1) * INNER],
                        wk_in, 16 * C, wk_hi)
            values_in(0, 0)
            values_in(0, 1)
            for c in range(C):
                split_w(wkv_h[:, c, INNER:2 * INNER], raw[:, (C + c) * INNER:(C + c + 1) * INNER],
                        wv_in, 16 * C, wv_hi)
            queries_hi(0, 0)
            for j in range(PAIRS):
                keys_hi(0, j)
                if j == 0:
                    queries_hi(0, 1)
                if j == 1:
                    exps(0, 0)
                if j == 2:
                    values_in(1, 0)
                if j == 3:
                    values_in(1, 1)
            split_w(wo_h[:, :, :], raw[:, 0:PAIRS * D].rearrange("p (j d) -> p j d", j=PAIRS),
                    wo_in, 16, wo_hi)
            for i in range(PAIRS // 2):
                values_out(0, i, 0)
                values_out(0, i, 1)
            with act.Fori(0, B - 2) as b:
                batch(b, True, True)
            batch(B - 2, True, False)
            batch(B - 1, False, False)

            act.wait_ge(x1_done, X0 + B)
            act.wait_ge(ffw_in, 64)
            act.activation(w_h[0][:, 0:GUW], raw[:, 0:GUW], ACT.Copy)
            act.activation(w_h[0][0:MS[0], GUW:GUW + 4 * D], raw[0:MS[0], GUW:GUW + 4 * D],
                           ACT.Copy)
            act.activation(w_h[0][0:MS[4], GUW + 4 * D:FW], raw[0:MS[4], GUW + 4 * D:FW],
                           ACT.Copy).then_inc(ffw_hi, 1)
            with act.Fori(0, B // 2) as i:
                for u in range(2):
                    b = 2 * i + u
                    act.wait_ge(xt_done, R0 + b + 1)
                    src = bT[u][:, 0:C * L].rearrange("p (c l) -> p c l", c=C)
                    act.activation(xn_h[:, :, bass.ds(b * L, L)], src, ACT.Copy
                                   ).then_inc(xn_hi_done, 1)
                    act.wait_ge(gated, G0 + b)
                    act.activation(xnT[u][:, :, :], src, ACT.Copy).then_inc(xn_copied, 1)
            act.wait_ge(route, 2)
            act.activation(ex[:, :, :], lg[:, :, :], ACT.Exp).then_inc(route_exp, 1)

            def expert(k, wt, shared, more):
                with act.Fori(0, G) as g:
                    for m in range(M6):
                        n = (k * G + g) * M6 + m
                        act.wait_ge(gate_mm, n + 1)
                        act.wait_ge(h_mul, n + 1)
                        act.activation(sl[0:MS[m], m % 2, :], gb[m % 2][0:MS[m], 0:GT], ACT.Silu
                                       ).then_inc(silu_done, 1)
                        if more and m in (2, 3):
                            if m == 2:
                                act.wait_ge(ffw_in, 64 * (k + 2))
                                act.wait_ge(down_mm, D0 + M6 * G * k)
                                act.activation(w_h[1 - wt][:, bass.ds(g * I, I)],
                                               raw[:, bass.ds(g * I, I)], ACT.Copy)
                            else:
                                cols = bass.ds(g * D + GUW, D)
                                act.activation(w_h[1 - wt][0:MS[0], cols], raw[0:MS[0], cols],
                                               ACT.Copy).then_inc(ffw_piece, 1)
                    if shared:
                        act.wait_ge(down_mm, D0 + (k * G + g + 1) * M6)
                        for c in range(C):
                            act.activation(accT[:, c, bass.ds(g * GT, GT)], yb[c][:, 0:GT],
                                           ACT.Copy).then_inc(y_out, 1)
                if more:
                    act.activation(w_h[1 - wt][0:MS[4], GUW + 4 * D:FW],
                                   raw[0:MS[4], GUW + 4 * D:FW], ACT.Copy).then_inc(ffw_hi, 1)

            expert(0, 0, True, True)
            expert(1, 1, False, True)
            expert(2, 0, False, True)
            expert(3, 1, False, True)
            expert(4, 0, False, False)

        @block.vector
        def _(dve):
            TILES = [(SR, r) for r in range(CT)] + [(L, CT)]

            def row_stats(t):
                dve.wait_ge(ctx_loaded, 16 * (t + 1))
                xt = x1[:, bass.ds(t, 1), :].rearrange("p a d -> p (a d)")
                for n, r in TILES:
                    i = dve.bn_stats(st[0:n, r, :], ctx_raw[:, r, :] if r < CT else xt)
                i.then_inc(stats, 1)
                dve.wait_ge(stats, t + 1)
                plain(dve)
                for n, r in TILES:
                    i = dve.bn_aggr(mv[0:n, r, :], st[0:n, r, :])
                i.then_inc(aggr, 1)
                dve.wait_ge(aggr, t + 1)
                dve.tensor_scalar(ve[:, 0:CT], mv[:, 0:CT, 1], EPS, None, ALU.add)
                dve.tensor_scalar(ve[0:L, CT:CT + 1], mv[0:L, CT, 1:2], EPS, None, ALU.add
                                  ).then_inc(var_eps, 1)

            def row_norm(t):
                dve.wait_ge(rstd_done, t + 1)
                if not (isinstance(t, int) and t == 0):
                    dve.wait_ge(kvt_done, 2 * t)
                xt = x1[:, bass.ds(t, 1), :].rearrange("p a d -> p (a d)")
                for n, r in TILES:
                    i = dve.tensor_scalar(rows[0:n, r, :], ctx_raw[:, r, :] if r < CT else xt,
                                          mv[0:n, r, 0:1], rstd[0:n, r:r + 1],
                                          ALU.subtract, ALU.mult)
                i.then_inc(lat_done, 1)
                dve.wait_ge(lat_done, t + 1)
                dve.bn_stats(lst[:, :], rows[0:L, CT, :]).then_inc(lstats, 1)
                dve.wait_ge(lstats, t + 1)
                plain(dve)
                dve.bn_aggr(lmv[:, :], lst[:, :]).then_inc(laggr, 1)
                dve.wait_ge(laggr, t + 1)
                dve.tensor_scalar(lve[:, :], lmv[:, 1:2], EPS, None, ALU.add
                                  ).then_inc(lvar_eps, 1)

            def latent_norm(t):
                dve.wait_ge(lrstd_done, t + 1)
                dve.tensor_scalar(rows[0:L, CT, :], rows[0:L, CT, :], lmv[:, 0:1], lrstd[:, 0:1],
                                  ALU.subtract, ALU.mult).then_inc(rows_done, 1)

            def split_lo(dst, full, hi, waits, done):
                for s, at_least in waits:
                    dve.wait_ge(s, at_least)
                dve.tensor_tensor(dst, full, SPLIT(hi), ALU.subtract).then_inc(done, 1)

            def values_in_hi(t):
                dve.wait_ge(val_done, 2 * t + 2)
                if not (isinstance(t, int) and t == 0):
                    dve.wait_ge(vproj, PAIRS * t)
                dve.tensor_copy(kv_h[:, :, :], val[:, :, :]).then_inc(kv_hi_done, 1)

            def keys_lo(t, j):
                split_lo(k_l[:, j, :], bK[:, 0:KW], k_h[:, j, :],
                         [(k_hi_done, PAIRS * t + j + 1)], k_lo_done)

            def queries_lo(t, half):
                dve.wait_ge(q_hi_done, 2 * t + half + 1)
                js = slice(4 * half, 4 * half + 4)
                dve.scalar_tensor_tensor(q_l[:, js, :],
                                         bM[:, 0:4 * L].rearrange("p (j l) -> p j l", j=4),
                                         DH ** -0.5, SPLIT(q_h[:, js, :]), ALU.mult, ALU.subtract
                                         ).then_inc(q_lo_done, 1)

            def maxima(b, j):
                for u in range(2):
                    h = 2 * j + u
                    dve.wait_ge(scored, H * b + h + 1)
                    dve.tensor_reduce(nmax[:, h:h + 1], bS[u][0:L, 0:SK], AX.X, ALU.max,
                                      negate=True).then_inc(maxed, 1)

            def invert(b, h):
                dve.wait_ge(exped, S0 + H * b + h + 1)
                dve.reciprocal(rinv[:, h:h + 1], rsum[:, h:h + 1]).then_inc(inverted, 1)

            def turned_copy(b, h):
                dve.wait_ge(turned, T0 + H * b + h + 1)
                dve.wait_ge(pv_done, PAIRS * b + h // 2 + 1)
                dve.tensor_copy(probT[:, h % 4, :, :],
                                bT[h % 2][0:KR, 0:KT * L].rearrange("p (s l) -> p s l", s=KT)
                                ).then_inc(turned_out, 1)

            def heads_lo(b, half):
                js = slice(4 * half, 4 * half + 4)
                split_lo(o_l[:, js, :], bO[:, 0:4 * L].rearrange("p (j l) -> p j l", j=4),
                         o_h[:, js, :], [(o_hi_done, 2 * b + half + 1)], o_lo_done)

            def residual(b):
                dve.wait_ge(wo_done, W0 + b + 1)
                xb = x1[:, bass.ds(b, 1), :].rearrange("p a d -> p (a d)")
                dve.scalar_tensor_tensor(xb, bM[0:L, 0:D], tgate[0:L, 0:1], xb,
                                         ALU.mult, ALU.add).then_inc(x1_done, 1)
                dve.wait_ge(x1_done, X0 + b + 1)
                dve.bn_stats(ffn_st[:, bass.ds(b, 1), :].rearrange("p a s -> p (a s)"), xb
                             ).then_inc(fstats, 1)

            def batch(b, next1, next2):
                for j in range(PAIRS):
                    if j > 0:
                        maxima(b, j)
                        turned_copy(b, 2 * j - 2)
                        turned_copy(b, 2 * j - 1)
                        invert(b, 2 * j)
                        invert(b, 2 * j + 1)
                    if next1:
                        keys_lo(b + 1, j)
                        if j == 4:
                            queries_lo(b + 1, 0)
                    if j == 4:
                        heads_lo(b, 0)
                    if next2:
                        if j == 2:
                            row_stats(b + 2)
                        if j == 3:
                            row_norm(b + 2)
                        if j == 4:
                            latent_norm(b + 2)
                if next1:
                    queries_lo(b + 1, 1)
                turned_copy(b, H - 2)
                turned_copy(b, H - 1)
                heads_lo(b, 1)
                if next2:
                    values_in_hi(b + 2)
                if next1:
                    maxima(b + 1, 0)
                    invert(b + 1, 0)
                    invert(b + 1, 1)
                residual(b)

            dve.wait_ge(x_in, 16)
            row_stats(0)
            row_norm(0)
            latent_norm(0)
            for c in range(C):
                split_lo(wkv_l[:, c, 0:INNER], raw[:, c * INNER:(c + 1) * INNER],
                         wkv_h[:, c, 0:INNER], [(wk_hi, c + 1)], wk_lo)
            values_in_hi(0)
            queries_lo(0, 0)
            for j in range(PAIRS):
                keys_lo(0, j)
                if j == 0:
                    queries_lo(0, 1)
                    row_stats(1)
                if j == 1:
                    maxima(0, 0)
                    invert(0, 0)
                    invert(0, 1)
                    row_norm(1)
                    latent_norm(1)
            values_in_hi(1)
            dve.wait_ge(tanh_done, 1)
            with dve.Fori(0, B - 2) as b:
                batch(b, True, True)
            batch(B - 2, True, False)
            batch(B - 1, False, False)

            dve.wait_ge(fstats, B)
            for b in range(B):
                i = dve.bn_aggr(ffn_mv[:, b, :], ffn_st[:, b, :])
            i.then_inc(faggr, 1)
            dve.wait_ge(faggr, 1)
            dve.tensor_scalar(ffn_ve[:, :], ffn_mv[:, :, 1], EPS, None, ALU.add
                              ).then_inc(fve_done, 1)
            dve.wait_ge(frstd, 1)
            with dve.Fori(0, B // 2) as i:
                for u in range(2):
                    b = 2 * i + u
                    xb = x1[:, bass.ds(b, 1), :].rearrange("p a d -> p (a d)")
                    dve.wait_ge(xt_done, b + 1)
                    dve.tensor_scalar(xrow[u][:, :], xb,
                                      ffn_mv[:, bass.ds(b, 1), 0:1].rearrange("p a s -> p (a s)"),
                                      ffn_rstd[:, bass.ds(b, 1)],
                                      ALU.subtract, ALU.mult).then_inc(xrow_done, 1)
                for u in range(2):
                    b = 2 * i + u
                    tok = bass.ds(b * L, L)
                    split_lo(xn_l[:, :, tok], bT[u][:, 0:C * L].rearrange("p (c l) -> p c l", c=C),
                             xn_h[:, :, tok], [(xn_copied, b + 1)], xn_lo_done)

            step = [0]

            def routed(i):
                i.then_inc(route, 1)
                step[0] += 1
                dve.wait_ge(route, step[0])

            def over_e(ap):
                return ap.unsqueeze(2).broadcast_to((L, B, E))

            dve.wait_ge(gated, G0 + B)
            routed(dve.tensor_reduce(lmax[:, :], bM[0:L, 0:B * E].rearrange("p (b e) -> p b e", e=E),
                                     AX.X, ALU.max))
            routed(dve.tensor_tensor(lg[:, :, :], bM[0:L, 0:B * E].rearrange("p (b e) -> p b e", e=E),
                                     over_e(lmax[:, :]), ALU.subtract))
            dve.wait_ge(route_exp, 1)
            routed(dve.tensor_reduce(esum[:, :], ex[:, :, :], AX.X, ALU.add))
            routed(dve.reciprocal(wsum[:, :], esum[:, :]))
            routed(dve.tensor_tensor(sc[:, :, :], ex[:, :, :], over_e(wsum[:, :]), ALU.mult))
            for f in range(E):
                fs = lambda n: sc[:, :, f:f + 1].broadcast_to((L, B, n))
                i = dve.tensor_tensor(beat[:, f, :, 0:f + 1], fs(f + 1), sc[:, :, 0:f + 1],
                                      ALU.is_gt)
                if f < E - 1:
                    i = dve.tensor_tensor(beat[:, f, :, f + 1:E], fs(E - 1 - f),
                                          sc[:, :, f + 1:E], ALU.is_ge)
            routed(i)
            routed(dve.tensor_reduce(rank[:, :, :], beat[:, :, :, :].rearrange("p f b e -> p b e f"),
                                     AX.X, ALU.add))
            routed(dve.scalar_tensor_tensor(wsel[:, :, :], rank[:, :, :], 1.5, sc[:, :, :],
                                            ALU.is_lt, ALU.mult))
            routed(dve.tensor_reduce(esum[:, :], wsel[:, :, :], AX.X, ALU.add))
            routed(dve.tensor_scalar(esum[:, :], esum[:, :], 1e-20, None, ALU.add))
            routed(dve.reciprocal(wsum[:, :], esum[:, :]))
            routed(dve.tensor_tensor(comb[:, :, :].rearrange("p e b -> p b e"), wsel[:, :, :],
                                     over_e(wsum[:, :]), ALU.mult))
            assert step[0] == ROUTED

            def expert(k, wt, turn):
                shared = isinstance(k, int)
                if not shared:
                    dve.wait_ge(cb_in[wt], 16 * turn)
                    plain(dve)
                with dve.Fori(0, G) as g:
                    for m in range(M6):
                        n = (k * G + g) * M6 + m
                        dve.wait_ge(silu_done, n + 1)
                        dve.wait_ge(up_mm, n + 1)
                        dve.wait_ge(h_lo_done, n + 1)
                        dve.tensor_tensor(hf[0:MS[m], m % 2, :], ub[m % 2][0:MS[m], 0:GT],
                                          sl[0:MS[m], m % 2, :], ALU.mult).then_inc(h_mul, 1)
                        dve.wait_ge(h_mul, H0 + n + 1)
                        dve.wait_ge(down_mm, D0 + M6 * (k * G + g))
                        dve.tensor_copy(h_h[0:MS[m], m, :], hf[0:MS[m], m % 2, :]
                                        ).then_inc(h_hi_done, 1)
                    if not shared:
                        dve.wait_ge(down_mm, D0 + (k * G + g + 1) * M6)
                        dve.wait_ge(acc_done, A0 + C * ((k - 1) * G + g))
                        for c in range(C):
                            dve.tensor_tensor(ytmp[:, c, :], yb[c][:, 0:GT],
                                              cb[wt][:, bass.ds(g * GT, GT)], ALU.mult
                                              ).then_inc(y_out, 1)

            expert(0, 0, 0)
            dve.wait_ge(comb_t, 1)
            dve.tensor_copy(combT[:, :], bM[0:E * B, 0:L]).then_inc(comb_c, 1)
            with dve.Fori(0, E // 2) as i:
                expert(2 * i + 1, 1, i + 1)
                expert(2 * i + 2, 0, i + 1)

            with dve.Fori(0, B // 2) as i:
                for u in range(2):
                    b = 2 * i + u
                    dve.wait_ge(yt_done, b + 1)
                    xb = x1[:, bass.ds(b, 1), :].rearrange("p a d -> p (a d)")
                    dve.scalar_tensor_tensor(xb, bT[u][0:L, 0:D], tgate[0:L, 1:2], xb,
                                             ALU.mult, ALU.add).then_inc(fin, 1)

        @block.gpsimd
        def _(pool):
            pool.memset(ident[:, :], 0.0).then_inc(ident0, 1)
            pool.memset(neghalf[:, :], -0.5).then_inc(const_set, 1)
            pool.memset(val[:, :, SK:KW], 0.0).then_inc(const_set, 1)
            pool.memset(prob[:, :, SK:KW], 0.0).then_inc(const_set, 1)
            pool.wait_ge(ident0, 1)
            pool.affine_select(out=ident[:, :], in_=ident[:, :], compare_op=ALU.not_equal,
                               fill=1.0, base=0, pattern=[[-1, P]], channel_multiplier=1
                               ).then_inc(const_set, 1)
            for s, start in ((exped, S0), (turned, T0), (turned_out, C0), (pv_done, V0),
                             (o_lo_done, O0), (x1_done, X0), (wo_done, W0), (xt_done, R0),
                             (xn_lo_done, R0), (gated, G0), (h_mul, H0), (h_lo_done, H0),
                             (down_mm, D0), (y_out, Y0), (acc_done, A0)):
                pool.sem_inc(s, start)
            pool.wait_ge(const_set, 4)

            def power(dst, src, cols):
                return pool.tensor_tensor(dst, src, cols, ALU.pow)

            def row_rstd(t):
                pool.wait_ge(var_eps, t + 1)
                power(rstd[:, 0:CT], ve[:, 0:CT], neghalf[0:SR, 0:CT])
                power(rstd[0:L, CT:CT + 1], ve[0:L, CT:CT + 1], neghalf[0:L, 0:1]
                      ).then_inc(rstd_done, 1)

            def latent_rstd(t):
                pool.wait_ge(lvar_eps, t + 1)
                power(lrstd[:, :], lve[:, :], neghalf[0:L, 0:1]).then_inc(lrstd_done, 1)

            def normalise(b, j):
                for u in range(2):
                    h = 2 * j + u
                    pool.wait_ge(inverted, H * b + h + 1)
                    plain(pool)
                    pool.tensor_scalar(prob[:, h % 4, 0:SK], prob[:, h % 4, 0:SK],
                                       rinv[:, h:h + 1], 1.0, ALU.mult, ALU.mult
                                       ).then_inc(normed, 1)

            def queries_in(t):
                pool.wait_ge(val_done, 2 * t + 2)
                if not (isinstance(t, int) and t == 0):
                    pool.wait_ge(qproj, 2 * t)
                    plain(pool)
                pool.tensor_copy(xq[:, :, :], val[:, :, S:SK]).then_inc(xq_done, 1)

            def values_in_lo(t):
                pool.wait_ge(kv_hi_done, t + 1)
                pool.tensor_tensor(kv_l[:, :, :], val[:, :, :], SPLIT(kv_h[:, :, :]),
                                   ALU.subtract).then_inc(kv_lo_done, 1)

            def batch(b, next1, next2):
                for j in range(PAIRS):
                    if j > 0:
                        normalise(b, j)
                    if next2 and j == 2:
                        row_rstd(b + 2)
                    if next2 and j == 3:
                        latent_rstd(b + 2)
                if next2:
                    values_in_lo(b + 2)
                    queries_in(b + 2)
                if next1:
                    normalise(b + 1, 0)

            row_rstd(0)
            latent_rstd(0)
            queries_in(0)
            values_in_lo(0)
            for c in range(C):
                pool.wait_ge(wv_hi, c + 1)
                pool.tensor_tensor(wkv_l[:, c, INNER:2 * INNER],
                                   raw[:, (C + c) * INNER:(C + c + 1) * INNER],
                                   SPLIT(wkv_h[:, c, INNER:2 * INNER]), ALU.subtract
                                   ).then_inc(wv_lo, 1)
            row_rstd(1)
            normalise(0, 0)
            latent_rstd(1)
            values_in_lo(1)
            queries_in(1)
            pool.wait_ge(wo_hi, 1)
            pool.tensor_tensor(wo_l[:, :, :], raw[:, 0:PAIRS * D].rearrange("p (j d) -> p j d", j=PAIRS),
                               SPLIT(wo_h[:, :, :]), ALU.subtract).then_inc(wo_lo, 1)
            with pool.Fori(0, B - 2) as b:
                batch(b, True, True)
            batch(B - 2, True, False)
            batch(B - 1, False, False)

            pool.wait_ge(fve_done, 1)
            power(ffn_rstd[:, :], ffn_ve[:, :], neghalf[0:L, :]).then_inc(frstd, 1)
            pool.wait_ge(ffw_hi, 1)

            def lo_part(wt, n, cols):
                return pool.tensor_tensor(w_l[wt][0:n, cols], raw[0:n, cols],
                                          SPLIT(w_h[wt][0:n, cols]), ALU.subtract)

            lo_part(0, P, slice(0, GUW))
            lo_part(0, MS[0], slice(GUW, GUW + 4 * D))
            lo_part(0, MS[4], slice(GUW + 4 * D, FW)).then_inc(ffw_lo, 1)

            def expert(k, wt, shared, more):
                with pool.Fori(0, G) as g:
                    for m in range(M6):
                        n = (k * G + g) * M6 + m
                        pool.wait_ge(h_hi_done, n + 1)
                        pool.tensor_tensor(h_l[0:MS[m], m, :], hf[0:MS[m], m % 2, :],
                                           SPLIT(h_h[0:MS[m], m, :]), ALU.subtract
                                           ).then_inc(h_lo_done, 1)
                        if more and m == 3:
                            pool.wait_ge(ffw_piece, k * G + g + 1)
                            lo_part(1 - wt, P, bass.ds(g * I, I))
                            lo_part(1 - wt, MS[0], bass.ds(g * D + GUW, D))
                    if not shared:
                        for c in range(C):
                            acc = accT[:, c, bass.ds(g * GT, GT)]
                            pool.wait_ge(y_out, Y0 + C * (k * G + g) + c + 1)
                            pool.tensor_tensor(acc, acc, ytmp[:, c, :], ALU.add
                                               ).then_inc(acc_done, 1)
                if more:
                    pool.wait_ge(ffw_hi, k + 2)
                    lo_part(1 - wt, MS[4], slice(GUW + 4 * D, FW)).then_inc(ffw_lo, 1)

            expert(0, 0, True, True)
            expert(1, 1, False, True)
            expert(2, 0, False, True)
            expert(3, 1, False, True)
            expert(4, 0, False, False)


def kernel(x, ctx_1024, g_xattn, g_ffn, L0_xattn_Wq, L0_xattn_Wkv, L0_xattn_Wo, L0_xattn_ln1_w,
           L0_xattn_ln1_b, L0_xattn_ln2_w, L0_xattn_ln2_b, L0_ffn_gate_w, L0_ffn_eg, L0_ffn_eu,
           L0_ffn_ed, L0_ffn_sg, L0_ffn_su, L0_ffn_sd):
    import numpy as np
    import concourse.bacc as bacc
    from concourse.bass_utils import run_bass_kernel_spmd

    def experts(shared, routed):
        both = np.concatenate([np.asarray(shared)[None], np.asarray(routed)])
        return both.transpose(0, 2, 1)

    ln_wb = np.stack([np.asarray(a).reshape(-1, P) for a in (
        L0_xattn_ln1_w, L0_xattn_ln1_b, L0_xattn_ln2_w, L0_xattn_ln2_b)]).transpose(2, 0, 1)

    ins = [("x", x), ("ctx", ctx_1024), ("g_xattn", g_xattn), ("g_ffn", g_ffn),
           ("wq", L0_xattn_Wq), ("wkv", L0_xattn_Wkv), ("wo", L0_xattn_Wo),
           ("ln_wb", ln_wb),
           ("gate_wT", np.asarray(L0_ffn_gate_w).T),
           ("gateT", experts(L0_ffn_sg, L0_ffn_eg)), ("upT", experts(L0_ffn_su, L0_ffn_eu)),
           ("downT", experts(L0_ffn_sd, L0_ffn_ed))]
    nc = bacc.Bacc("TRN2", target_bir_lowering=False, num_devices=1)
    arrays, aps = {}, []
    for name, a in ins:
        a = np.ascontiguousarray(a)
        arrays[f"in_{name}"] = a
        aps.append(nc.dram_tensor(f"in_{name}", a.shape, mybir.dt.from_np(a.dtype),
                                  kind="ExternalInput").ap())
    shape = np.asarray(x).shape
    out = nc.dram_tensor("out_x", shape, F32, kind="ExternalOutput").ap()
    flamingo_block(nc, *aps, out)
    r = run_bass_kernel_spmd(nc, [arrays], core_ids=[0])
    return r.results[0]["out_x"]
```

```python
from contextlib import ExitStack

import concourse.bass as bass
from concourse import mybir

ALU = mybir.AluOpType
ACT = mybir.ActivationFunctionType
AX = mybir.AxisListType
F32 = mybir.dt.float32
F32R = mybir.dt.float32r

EPS = 1e-5
P = 128
DH = 64
KT = 4
CT = 3
PAIRS = 8
GB = 4


def flamingo_block(nc, x, ctx_in, g_xattn, g_ffn, Wq, Wkv, Wo, ln_wb,
                   gate_wT, gateT, upT, downT, out):
    B, L, D = x.shape
    S = ctx_in.shape[1]
    INNER = Wq.shape[1]
    E1, _, I = gateT.shape
    E = E1 - 1
    C = D // P
    SK = S + L
    KW = (SK + KT - 1) // KT * KT
    KR = KW // KT
    SR = S // CT
    H = INNER // DH
    assert H == 2 * PAIRS and S % CT == 0 and KW - SK == 1 and C == 2
    N = B * L
    GT = GB * L
    G = B // GB
    MS = [116] * 4 + [112] * 2
    MO = [sum(MS[:m]) for m in range(6)]
    M6 = len(MS)
    assert sum(MS) == I
    GUW = 2 * C * I
    FW = GUW + M6 * D
    SPLIT = lambda t: t.bitcast(F32)

    with ExitStack() as life:
        def sem(name):
            return life.enter_context(nc.semaphore(name))

        def sb(stack, name, shape, dt=F32):
            return stack.enter_context(nc.sbuf_tensor(name, shape, dt))

        x1 = sb(life, "x1", [L, B, D])
        raw = sb(life, "raw", [P, FW])
        ident = sb(life, "ident", [P, P])
        gates = sb(life, "gates", [P, 2])
        tgate = sb(life, "tgate", [P, 2])
        gw = sb(life, "gw", [P, C, E])
        neghalf = sb(life, "neghalf", [P, CT])
        fst = sb(life, "fst", [L, 6])
        fmv = sb(life, "fmv", [L, 2])
        fve = sb(life, "fve", [L, 1])
        frstd = sb(life, "frstd", [L, 1])
        frow = sb(life, "frow", [L, D])
        xnT = sb(life, "xnT", [P, C, N])
        cb = [xnT[:, i, :] for i in range(2)]

        one = ExitStack()
        wkv_h = sb(one, "wkv_h", [P, C, 2 * INNER], F32R)
        wkv_l = sb(one, "wkv_l", [P, C, 2 * INNER], F32R)
        wq = sb(one, "wq", [P, C, INNER])
        lnw = sb(one, "lnw", [P, 4, C])
        ctx_raw = sb(one, "ctx_raw", [SR, CT, D])
        rows = sb(one, "rows", [SR, CT + 1, D])
        st = sb(one, "st", [SR, CT + 1, 6])
        mv = sb(one, "mv", [SR, CT + 1, 2])
        ve = sb(one, "ve", [SR, CT + 1])
        rstd = sb(one, "rstd", [SR, CT + 1])
        lst = sb(one, "lst", [L, 6])
        lmv = sb(one, "lmv", [L, 2])
        lve = sb(one, "lve", [L, 1])
        lrstd = sb(one, "lrstd", [L, 1])
        val = sb(one, "val", [P, C, KW])
        kv_h = sb(one, "kv_h", [P, C, KW], F32R)
        kv_l = sb(one, "kv_l", [P, C, KW], F32R)
        xq = sb(one, "xq", [P, C, L])
        keys = sb(one, "keys", [P, PAIRS, 2, KW], F32R)
        wo_h = sb(one, "wo_h", [P, PAIRS, D], F32R)
        wo_l = sb(one, "wo_l", [P, PAIRS, D], F32R)
        q_h = sb(one, "q_h", [P, PAIRS, 2, L], F32R)
        q_l = sb(one, "q_l", [P, PAIRS, L], F32R)
        v = sb(one, "v", [KR, KT, INNER])
        nmax = sb(one, "nmax", [L, H])
        rsum = sb(one, "rsum", [L, H])
        rinv = sb(one, "rinv", [L, H])
        prob = sb(one, "prob", [L, 4, KW])
        probT = sb(one, "probT", [KR, 4, KT, L])
        o_h = sb(one, "o_h", [P, PAIRS, L], F32R)
        o_l = sb(one, "o_l", [P, PAIRS, L], F32R)
        one.close()

        two = ExitStack()
        w_h0 = sb(two, "w_h0", [P, FW], F32R)
        w_l0 = sb(two, "w_l0", [P, FW], F32R)
        xn_h = sb(two, "xn_h", [P, C, N], F32R)
        xn_l = sb(two, "xn_l", [P, C, N], F32R)
        w_h = [w_h0, sb(two, "w_h1", [P, FW], F32R)]
        w_l = [w_l0, sb(two, "w_l1", [P, FW], F32R)]
        accT = sb(two, "accT", [P, C, N])
        lg = sb(two, "lg", [L, B, E])
        lmax = sb(two, "lmax", [L, B])
        ex = sb(two, "ex", [L, B, E])
        esum = sb(two, "esum", [L, B])
        sc = sb(two, "sc", [L, B, E])
        beat = sb(two, "beat", [L, E, B, E])
        rank = sb(two, "rank", [L, B, E])
        wsel = sb(two, "wsel", [L, B, E])
        wsum = sb(two, "wsum", [L, B])
        comb = sb(two, "comb", [L, E, B])
        combT = sb(two, "combT", [E * B, L])
        sl = sb(two, "sl", [P, 2, GT])
        hf = sb(two, "hf", [P, 2, GT])
        h_h = sb(two, "h_h", [P, M6, GT], F32R)
        h_l = sb(two, "h_l", [P, M6, GT], F32R)
        ytmp = sb(two, "ytmp", [P, C, GT])
        two.close()
        comb_dram = nc.dram_tensor("comb_dram", (E * B, L), F32, kind="Internal").ap()

        bank = [life.enter_context(nc.psum_tensor(f"bank{i}", [P, 512], F32)) for i in range(8)]
        bS = bank[0:2]
        bT = bank[2:4]
        bK, bV, bO, bM = bank[4:8]
        gb, ub, yb = bank[0:2], bank[4:6], [bank[6], bank[2]]
        rb = [bank[3], bank[7]]

        x_in, x_rest_in, ctx_loaded, small_in, wq_in, out_done = map(sem, (
            "x_in", "x_rest_in", "ctx_loaded", "small_in", "wq_in", "out_done"))
        wk_in, wv_in, wo_in = map(sem, ("wk_in", "wv_in", "wo_in"))
        wk_hi, wk_lo, wv_hi, wv_lo, wo_hi, wo_lo = map(sem, (
            "wk_hi", "wk_lo", "wv_hi", "wv_lo", "wo_hi", "wo_lo"))
        ident0, const_set, tanh_done = map(sem, ("ident0", "const_set", "tanh_done"))
        stats, aggr, var_eps, rstd_done, lat_done, ctx_norm = map(sem, (
            "stats", "aggr", "var_eps", "rstd_done", "lat_done", "ctx_norm"))
        lstats, laggr, lvar_eps, lrstd_done, rows_done = map(sem, (
            "lstats", "laggr", "lvar_eps", "lrstd_done", "rows_done"))
        kvt_done, val_done, kv_hi_done, kv_lo_done, xq_done = map(sem, (
            "kvt_done", "val_done", "kv_hi_done", "kv_lo_done", "xq_done"))
        kproj, k_hi_done, k_lo_done, vproj, v_out, qproj, q_hi_done, q_lo_done = map(sem, (
            "kproj", "k_hi_done", "k_lo_done", "vproj", "v_out", "qproj", "q_hi_done", "q_lo_done"))
        scored, maxed, exped, inverted, normed, turned, q_dup_done = map(sem, (
            "scored", "maxed", "exped", "inverted", "normed", "turned", "q_dup_done"))
        turned_out = [sem(f"turned_out{u}") for u in range(2)]
        pv_done, o_hi_done, o_lo_done, wo_done, x1_done = map(sem, (
            "pv_done", "o_hi_done", "o_lo_done", "wo_done", "x1_done"))
        fstats, faggr, fve_done, frstd_done, frow_done, ft_done, xnT_done = map(sem, (
            "fstats", "faggr", "fve_done", "frstd_done", "frow_done", "ft_done", "xnT_done"))
        xn_hi_done, xn_lo_done, gated = map(sem, ("xn_hi_done", "xn_lo_done", "gated"))
        route, route_exp, comb_t, comb_c, comb_out = map(sem, (
            "route", "route_exp", "comb_t", "comb_c", "comb_out"))
        cb_in = [sem(f"cb_in{i}") for i in range(2)]
        ffw_in, ffw_hi, ffw_lo, gw_in = map(sem, ("ffw_in", "ffw_hi", "ffw_lo", "gw_in"))
        gate_mm, up_mm, silu_done, h_mul, h_hi_done, h_lo_done, down_mm, y_out, acc_done = map(sem, (
            "gate_mm", "up_mm", "silu_done", "h_mul", "h_hi_done", "h_lo_done", "down_mm", "y_out",
            "acc_done"))
        yt_done, fin, waited = map(sem, ("yt_done", "fin", "waited"))

        S0 = 1
        T0 = 3
        C0 = 1
        V0 = 2
        O0 = 1
        X0 = 1
        W0 = 1
        F0 = 1
        H0 = 2
        D0 = 1
        Y0 = 1
        A0 = 1

        ROUTED = 12

        def piece(g):
            return (P, bass.ds(g * I, I)), (MS[0], bass.ds(g * D + GUW, D))
        LAST = ((MS[4], slice(GUW + 4 * D, FW)),)
        PIECES = 5

        def plain(eng):
            eng.sem_inc(waited, 1)

        def value_bank(t, n):
            return bK if n == PAIRS - 1 or isinstance(t, int) and t == 0 and n % 2 else bV

        def key_bank(t, j):
            return bV if j == 0 or isinstance(t, int) and t == 0 and j % 2 == 0 else bK

        HP = PAIRS // 2

        def wo_raw(n):
            return raw[:, n * HP * D:(n + 1) * HP * D].rearrange("p (j d) -> p j d", j=HP)

        HEAD = [slice(DH * u, DH * (u + 1)) for u in range(2)]

        block = life.enter_context(nc.Block())

        @block.sync
        def _(sp):
            def load_ctx(t):
                if not (isinstance(t, int) and t == 0):
                    sp.wait_ge(ctx_norm, CT * t)
                sp.dma_start(ctx_raw[:, :, :],
                             ctx_in[bass.ds(t, 1), :, :].rearrange("a (c p) d -> p (a c) d", p=SR)
                             ).then_inc(ctx_loaded, 16)

            load_ctx(0)
            sp.dma_start(x1[:, 0:2, :], x[0:2, :, :].rearrange("b l d -> l b d")
                         ).then_inc(x_in, 16)
            sp.dma_start(lnw[:, :, :], ln_wb).then_inc(small_in, 16)
            sp.dma_start(gates[:, 0:1], g_xattn.rearrange("(a n) -> a n", a=1).broadcast_to((P, 1))
                         ).then_inc(small_in, 16)
            sp.dma_start(gates[:, 1:2], g_ffn.rearrange("(a n) -> a n", a=1).broadcast_to((P, 1))
                         ).then_inc(small_in, 16)
            for c in range(C):
                sp.dma_start(raw[:, c * INNER:(c + 1) * INNER],
                             Wkv[c * P:(c + 1) * P, 0:INNER]).then_inc(wk_in, 16)
            sp.dma_start(wq[:, :, :], Wq.rearrange("(c p) n -> p c n", p=P)).then_inc(wq_in, 16)
            for c in range(C):
                sp.dma_start(raw[:, (C + c) * INNER:(C + c + 1) * INNER],
                             Wkv[c * P:(c + 1) * P, INNER:2 * INNER]).then_inc(wv_in, 16)
            load_ctx(1)
            sp.wait_ge(wk_lo, C)
            sp.dma_start(raw[:, 0:PAIRS * D].rearrange("p (j d) -> p j d", j=PAIRS),
                         Wo.rearrange("(j p) d -> p j d", p=P)).then_inc(wo_in, 16)
            sp.dma_start(gw[:, :, :], gate_wT.rearrange("(c p) e -> p c e", p=P)
                         ).then_inc(gw_in, 16)
            sp.dma_start(x1[:, 2:B, :], x[2:B, :, :].rearrange("b l d -> l b d")
                         ).then_inc(x_rest_in, 16)
            with sp.Fori(2, B) as t:
                load_ctx(t)

            def load_expert(k):
                gate = gateT[k, :, :].rearrange("(c p) i -> p c i", p=P)
                up = upT[k, :, :].rearrange("(c p) i -> p c i", p=P)
                for n, w in enumerate((gate, up)):
                    sp.dma_start(raw[:, n * C * I:(n + 1) * C * I].rearrange("p (c i) -> p c i", c=C),
                                 w).then_inc(ffw_in, 16)
                for m0, m1 in ((0, 4), (4, M6)):
                    sp.dma_start(
                        raw[0:MS[m0], GUW + m0 * D:GUW + m1 * D].rearrange("p (m d) -> p m d", d=D),
                        downT[k, MO[m0]:MO[m0] + (m1 - m0) * MS[m0], :].rearrange(
                            "(m p) d -> p m d", p=MS[m0])).then_inc(ffw_in, 16)

            def load_comb(k):
                sp.dma_start(cb[k % 2][:, :],
                             comb_dram[(k - 1) * B:k * B, :].rearrange("b l -> (b l)")
                             .partition_broadcast(P)).then_inc(cb_in[k % 2], 16)

            sp.wait_ge(wv_lo, C)
            sp.wait_ge(wo_lo, 2)
            load_expert(0)
            sp.wait_ge(ffw_lo, PIECES)
            load_expert(1)
            sp.wait_ge(comb_c, 1)
            sp.dma_start(comb_dram, combT[:, :]).then_inc(comb_out, 16)
            sp.wait_ge(comb_out, 16)
            sp.wait_ge(xn_lo_done, G)
            load_comb(1)
            load_comb(2)
            for k in range(2, E1):
                sp.wait_ge(ffw_lo, PIECES * k)
                load_expert(k)
                if k >= 3:
                    sp.wait_ge(y_out, Y0 + C * G * (k - 1))
                    load_comb(k)
            QB = B // 4
            for q in range(4):
                sp.wait_ge(fin, QB * (q + 1))
                sp.dma_start(out[q * QB:(q + 1) * QB, :, :].rearrange("b l d -> l b d"),
                             x1[:, q * QB:(q + 1) * QB, :]).then_inc(out_done, 16)
            sp.wait_ge(out_done, 64)

        @block.tensor
        def _(pe):
            def three(out_ap, w_hi, w_lo, m_hi, m_lo, start, stop):
                pe.matmul(out_ap, w_hi, m_hi, start=start, stop=False)
                pe.matmul(out_ap, w_hi, m_lo, start=False, stop=False)
                return pe.matmul(out_ap, w_lo, m_hi, start=False, stop=stop)

            def turn_rows(t, c, bank_free):
                pe.wait_ge(rows_done, t + 1)
                for s, at_least in bank_free:
                    pe.wait_ge(s, at_least)
                for r in range(CT + 1):
                    n = SR if r < CT else L
                    mm = pe.transpose(bM[:, r * SR:r * SR + n], rows[0:n, r, c * P:(c + 1) * P],
                                      ident[0:n, 0:n])
                mm.then_inc(kvt_done, 1)

            def project_q(t, half, bank_free):
                pe.wait_ge(xq_done, t + 1)
                for s, at_least in bank_free:
                    pe.wait_ge(s, at_least)
                for i in range(4):
                    j = 4 * half + i
                    for c in range(C):
                        mm = pe.matmul(bM[:, i * L:(i + 1) * L], wq[:, c, j * P:(j + 1) * P],
                                       xq[:, c, :], start=(c == 0), stop=(c == C - 1))
                mm.then_inc(qproj, 1)

            def project_k(t, j):
                if j == 0:
                    pe.wait_ge(kv_lo_done, t + 1)
                    if not (isinstance(t, int) and t == 0):
                        pe.wait_ge(v_out, PAIRS * t - 1)
                elif j == 1:
                    if not (isinstance(t, int) and t == 0):
                        pe.wait_ge(v_out, PAIRS * t)
                elif not (isinstance(t, int) and t == 0):
                    pe.wait_ge(k_lo_done, PAIRS * t + j)
                else:
                    pe.wait_ge(k_lo_done, j - 1)
                for c in range(C):
                    mm = three(key_bank(t, j)[:, 0:KW], wkv_h[:, c, j * P:(j + 1) * P],
                               wkv_l[:, c, j * P:(j + 1) * P], kv_h[:, c, :], kv_l[:, c, :],
                               c == 0, c == C - 1)
                mm.then_inc(kproj, 1)

            def project_v(t, i, half):
                part = 2 * i + half
                to = value_bank(t, part)
                if isinstance(t, int) and t == 0:
                    if part < 2:
                        pe.wait_ge(k_lo_done, PAIRS)
                    else:
                        pe.wait_ge(v_out, part - 1)
                elif part == PAIRS - 1:
                    pe.wait_ge(k_lo_done, PAIRS * (t + 1))
                elif part > 0:
                    pe.wait_ge(v_out, PAIRS * t + part)
                for n in range(2):
                    for c in range(C):
                        s = 2 * half + n
                        cols = slice(INNER + 2 * P * i, INNER + 2 * P * (i + 1))
                        keys = slice(s * KR, (s + 1) * KR)
                        mm = three(to[0:KR, n * 2 * P:(n + 1) * 2 * P], kv_h[:, c, keys],
                                   kv_l[:, c, keys], wkv_h[:, c, cols], wkv_l[:, c, cols],
                                   c == 0, c == C - 1)
                mm.then_inc(vproj, 1)

            def scores(b, j):
                pe.wait_ge(k_lo_done, PAIRS * b + j + 1)
                pe.wait_ge(q_lo_done, 2 * b + j // 4 + 1)
                pe.wait_ge(q_dup_done, 2 * b + j // 4 + 1)
                for u in range(2):
                    pe.wait_ge(exped, H * b + 2 * j + u)
                    pe.matmul(bS[u][0:L, 0:KW], q_h[:, j, u, :], keys[:, j, u, :],
                              start=True, stop=False)
                    pe.matmul(bS[u][0:L, 0:KW], q_l[HEAD[u], j, :], keys[HEAD[u], j, u, :],
                              start=False, stop=True).then_inc(scored, 1)

            def turn(b, j):
                for u in range(2):
                    n = H * b + 2 * j + u
                    pe.wait_ge(normed, n + 1)
                    pe.wait_ge(turned_out[u], PAIRS * b + j + 1)
                    for s in range(KT):
                        mm = pe.transpose(bT[u][0:KR, s * L:(s + 1) * L],
                                          prob[:, (2 * j + u) % 4, s * KR:(s + 1) * KR],
                                          ident[0:L, 0:L])
                    mm.then_inc(turned, 1)

            def weigh(b, j):
                for u in range(2):
                    pe.wait_ge(turned_out[u], C0 + PAIRS * b + j + 1)
                if j % 2 == 0:
                    pe.wait_ge(v_out, PAIRS * b + j + 2)
                if j % 4 == 0:
                    pe.wait_ge(o_lo_done, O0 + 2 * b + j // 4)
                for s in range(KT):
                    for u in range(2):
                        mm = pe.matmul(bO[DH * u:DH * (u + 1), (j % 4) * L:(j % 4 + 1) * L],
                                       v[:, s, P * j + DH * u:P * j + DH * (u + 1)],
                                       probT[:, (2 * j + u) % 4, s, :],
                                       start=(s == 0), stop=(s == KT - 1))
                mm.then_inc(pv_done, 1)

            def project_out(b, bank_free):
                if isinstance(b, int) and b == 0:
                    pe.wait_ge(wo_lo, 2)
                pe.wait_ge(o_lo_done, O0 + 2 * b + 2)
                for s, at_least in bank_free:
                    pe.wait_ge(s, at_least)
                for j in range(PAIRS):
                    mm = three(bM[0:L, 0:D], o_h[:, j, :], o_l[:, j, :], wo_h[:, j, :],
                               wo_l[:, j, :], j == 0, j == PAIRS - 1)
                mm.then_inc(wo_done, 1)

            def turn_ffn(b, bank_free):
                pe.wait_ge(frow_done, b + 1)
                for s, at_least in bank_free:
                    pe.wait_ge(s, at_least)
                for c in range(C):
                    mm = pe.transpose(bM[:, c * L:(c + 1) * L], frow[:, c * P:(c + 1) * P],
                                      ident[0:L, 0:L])
                mm.then_inc(ft_done, 1)

            def batch(b, before, next1, next2):
                for j in range(PAIRS):
                    if j > 0:
                        scores(b, j)
                        if not next1 and j > 1:
                            weigh(b, j - 2)
                        turn(b, j - 1)
                    if next1:
                        project_k(b + 1, j)
                        if j >= 2:
                            project_v(b + 1, (j - 2) // 2, j % 2)
                    if next1 and j == 1:
                        project_q(b + 1, 0, [(x1_done, X0 + b)])
                    if next1 and j == PAIRS - 1:
                        project_q(b + 1, 1, [(val_done, 2 * b + 6)] if next2
                                  else [(xnT_done, b)])
                    if j > 0 and next1:
                        weigh(b, j - 1)
                    if before and j == 4:
                        turn_ffn(b - 1, [(q_lo_done, 2 * b + 3)] if next1 else [])
                    if next2 and j == 5:
                        turn_rows(b + 2, 0, [(xnT_done, b)] if before else [(q_lo_done, 2 * b + 3)])
                    if next2 and j == 6:
                        turn_rows(b + 2, 1, [(val_done, 2 * b + 5)])
                if not next1:
                    weigh(b, PAIRS - 2)
                turn(b, PAIRS - 1)
                if next1:
                    project_v(b + 1, 3, 0)
                weigh(b, PAIRS - 1)
                if next1:
                    project_v(b + 1, 3, 1)
                    scores(b + 1, 0)
                project_out(b, [(q_lo_done, 2 * b + 4)] if next1 else [(xnT_done, b)])

            pe.wait_ge(const_set, 4)
            turn_rows(0, 0, [])
            turn_rows(0, 1, [(val_done, 1)])
            pe.wait_ge(wq_in, 16)
            project_q(0, 0, [(val_done, 2)])
            pe.wait_ge(wk_lo, C)
            for j in range(PAIRS):
                project_k(0, j)
                if j == 0:
                    project_q(0, 1, [(q_lo_done, 1)])
            pe.wait_ge(wv_lo, C)
            for i in range(PAIRS // 2):
                project_v(0, i, 0)
                if i == 0:
                    scores(0, 0)
                project_v(0, i, 1)
                if i == 1:
                    turn_rows(1, 0, [(q_lo_done, 2)])
                if i == 2:
                    turn_rows(1, 1, [(val_done, 3)])
            batch(0, False, True, True)
            with pe.Fori(1, B - 2) as b:
                batch(b, True, True, True)
            batch(B - 2, True, True, False)
            batch(B - 1, True, False, False)

            def hidden(k, wt, g, m):
                n = (k * G + g) * M6 + m
                pe.wait_ge(h_mul, n + 1)
                if m == 0:
                    pe.wait_ge(ffw_lo, PIECES * k + PIECES - 1)
                    if isinstance(k, int):
                        pe.wait_ge(xn_lo_done, g + 1)
                for part, to, done in ((0, gb, gate_mm), (1, ub, up_mm)):
                    for c in range(C):
                        cols = slice((C * part + c) * I + MO[m], (C * part + c) * I + MO[m] + MS[m])
                        tok = bass.ds(g * GT, GT)
                        mm = three(to[m % 2][0:MS[m], 0:GT], w_h[wt][:, cols], w_l[wt][:, cols],
                                   xn_h[:, c, tok], xn_l[:, c, tok], c == 0, c == C - 1)
                    mm.then_inc(done, 1)

            def down(k, wt, g, m):
                n = (k * G + g) * M6 + m
                pe.wait_ge(h_lo_done, H0 + n + 1)
                if m == 0:
                    pe.wait_ge(y_out, Y0 + C * (k * G + g))
                if m == 4:
                    pe.wait_ge(ffw_lo, PIECES * (k + 1))
                for c in range(C):
                    cols = slice(GUW + m * D + c * P, GUW + m * D + (c + 1) * P)
                    mm = three(yb[c][:, 0:GT], w_h[wt][0:MS[m], cols], w_l[wt][0:MS[m], cols],
                               h_h[0:MS[m], m, :], h_l[0:MS[m], m, :], m == 0, m == M6 - 1)
                mm.then_inc(down_mm, 1)

            def group(k, wt, g):
                for m in range(M6):
                    hidden(k, wt, g, m)
                    if 1 <= m < M6 - 2:
                        down(k, wt, g, m - 1)
                for m in range(M6 - 3, M6):
                    down(k, wt, g, m)

            def expert(k, wt):
                with pe.Fori(0, G) as g:
                    group(k, wt, g)

            with pe.Fori(0, G // 2) as g:
                group(0, 0, g)
            turn_ffn(B - 1, [])
            pe.wait_ge(gw_in, 16)
            for b in range(B):
                if b == B - 1:
                    pe.wait_ge(xnT_done, B)
                for c in range(C):
                    mm = pe.matmul(bank[3][0:L, b * E:(b + 1) * E], xnT[:, c, b * L:(b + 1) * L],
                                   gw[:, c, :], start=(c == 0), stop=(c == C - 1))
            mm.then_inc(gated, 1)
            with pe.Fori(G // 2, G) as g:
                group(0, 0, g)
            pe.wait_ge(route, ROUTED)
            pe.transpose(bM[0:E * B, 0:L], comb[:, :, :].rearrange("l e b -> l (e b)"),
                         ident[0:L, 0:L]).then_inc(comb_t, 1)
            with pe.Fori(0, E // 2) as i:
                expert(2 * i + 1, 1)
                expert(2 * i + 2, 0)

            for b in range(B):
                u = b % 2
                pe.wait_ge(acc_done, A0 + C * (G * (E - 1) + b // GB + 1))
                if b >= 2:
                    pe.wait_ge(fin, b - 1)
                for c in range(C):
                    mm = pe.transpose(rb[u][0:L, c * P:(c + 1) * P],
                                      accT[:, c, b * L:(b + 1) * L], ident[:, :])
                mm.then_inc(yt_done, 1)

        @block.scalar
        def _(act):
            def split_w(dst, src, loaded, at_least, done):
                act.wait_ge(loaded, at_least)
                act.activation(dst, src, ACT.Copy).then_inc(done, 1)

            def values_in(t, c):
                act.wait_ge(kvt_done, 2 * t + c + 1)
                if not (isinstance(t, int) and t == 0):
                    act.wait_ge(kv_hi_done, t)
                    act.wait_ge(kv_lo_done, t)
                    act.wait_ge(xq_done, t)
                act.activation(val[:, c, 0:S], bM[:, 0:S], ACT.Identity,
                               bias=lnw[:, 1, c:c + 1], scale=lnw[:, 0, c:c + 1])
                act.activation(val[:, c, S:SK], bM[:, S:SK], ACT.Identity,
                               bias=lnw[:, 3, c:c + 1], scale=lnw[:, 2, c:c + 1]
                               ).then_inc(val_done, 1)

            def keys_hi(t, j):
                act.wait_ge(kproj, PAIRS * t + j + 1)
                for u in range(2):
                    act.activation(keys[HEAD[u], j, u, :], key_bank(t, j)[HEAD[u], 0:KW], ACT.Copy
                                   ).then_inc(k_hi_done, 1)

            def values_out(t, i, half):
                act.wait_ge(vproj, PAIRS * t + 2 * i + half + 1)
                if not (isinstance(t, int) and t == 0):
                    act.wait_ge(pv_done, V0 + PAIRS * (t - 1) + 2 * i + 2)
                src = value_bank(t, 2 * i + half)
                act.activation(v[:, 2 * half:2 * half + 2, 2 * P * i:2 * P * (i + 1)],
                               src[0:KR, :].rearrange("p (s n) -> p s n", s=2), ACT.Copy
                               ).then_inc(v_out, 1)

            def queries_hi(t, half):
                act.wait_ge(qproj, 2 * t + half + 1)
                js = slice(4 * half, 4 * half + 4)
                for u in range(2):
                    i = act.activation(q_h[HEAD[u], js, u, :],
                                       bM[HEAD[u], 0:4 * L].rearrange("p (j l) -> p j l", j=4),
                                       ACT.Copy, scale=DH ** -0.5)
                i.then_inc(q_hi_done, 1)

            def queries_dup(t, half):
                js = slice(4 * half, 4 * half + 4)
                act.wait_ge(q_hi_done, 2 * t + half + 1)
                for u in range(2):
                    i = act.activation(q_h[HEAD[1 - u], js, u, :], SPLIT(q_h[HEAD[u], js, u, :]),
                                       ACT.Copy)
                i.then_inc(q_dup_done, 1)

            def turned_copy(b, j):
                act.wait_ge(turned, T0 + H * b + 2 * j + 1)
                act.wait_ge(pv_done, PAIRS * b + j + 1)
                act.activation(probT[:, 2 * j % 4, :, :],
                               bT[0][0:KR, 0:KT * L].rearrange("p (s l) -> p s l", s=KT), ACT.Copy
                               ).then_inc(turned_out[0], 1)

            def exps(b, j, copy=False):
                for u in range(2):
                    if copy and u == 1:
                        turned_copy(b, j - 1)
                    h = 2 * j + u
                    act.wait_ge(maxed, H * b + h + 1)
                    act.wait_ge(turned, H * b + h)
                    act.activation(prob[:, h % 4, 0:SK], bS[u][0:L, 0:SK], ACT.Exp,
                                   bias=nmax[:, h:h + 1], accum_out=rsum[:, h:h + 1]
                                   ).then_inc(exped, 1)

            def heads_hi(b, half):
                act.wait_ge(pv_done, V0 + PAIRS * b + 4 * half + 4)
                act.wait_ge(wo_done, W0 + b)
                act.activation(o_h[:, 4 * half:4 * half + 4, :],
                               bO[:, 0:4 * L].rearrange("p (j l) -> p j l", j=4), ACT.Copy
                               ).then_inc(o_hi_done, 1)

            def residual_out(b):
                act.wait_ge(ft_done, F0 + b + 1)
                act.activation(xnT[:, :, bass.ds(b * L, L)],
                               bM[:, 0:C * L].rearrange("p (c l) -> p c l", c=C), ACT.Copy
                               ).then_inc(xnT_done, 1)

            def weights_hi(wt, parts):
                for n, cols in parts:
                    i = act.activation(w_h[wt][0:n, cols], raw[0:n, cols], ACT.Copy)
                i.then_inc(ffw_hi, 1)

            def batch(b, before, next1, next2):
                for j in range(PAIRS):
                    if j > 0:
                        exps(b, j, True)
                    if before and j == 5:
                        residual_out(b - 1)
                    if isinstance(b, int) and b == 0 and j in (1, 2):
                        split_w(wo_h[:, HP * (j - 1):HP * j, :], wo_raw(j - 1), wo_in, 16, wo_hi)
                    if not next1 and 1 <= j <= PIECES:
                        if j == 1:
                            act.wait_ge(ffw_in, 64)
                            act.wait_ge(vproj, PAIRS * B)
                            act.wait_ge(qproj, 2 * B)
                        weights_hi(0, piece(j - 1) if j < PIECES else LAST)
                    if next1:
                        keys_hi(b + 1, j)
                        if j >= 2:
                            values_out(b + 1, (j - 2) // 2, j % 2)
                        if j == 3:
                            queries_hi(b + 1, 0)
                        if j == 4:
                            queries_dup(b + 1, 0)
                    if j == (4 if next1 else 5):
                        heads_hi(b, 0)
                    if next2 and j >= 5 and j < 7:
                        values_in(b + 2, j - 5)
                if next1:
                    queries_hi(b + 1, 1)
                turned_copy(b, PAIRS - 1)
                if next1:
                    queries_dup(b + 1, 1)
                heads_hi(b, 1)
                if next1:
                    values_out(b + 1, 3, 0)
                    values_out(b + 1, 3, 1)
                    exps(b + 1, 0)

            act.wait_ge(small_in, 48)
            act.wait_ge(const_set, 4)
            act.activation(tgate[:, :], gates[:, :], ACT.Tanh).then_inc(tanh_done, 1)
            for c in range(C):
                split_w(wkv_h[:, c, 0:INNER], raw[:, c * INNER:(c + 1) * INNER],
                        wk_in, 16 * C, wk_hi)
            values_in(0, 0)
            values_in(0, 1)
            for c in range(C):
                split_w(wkv_h[:, c, INNER:2 * INNER], raw[:, (C + c) * INNER:(C + c + 1) * INNER],
                        wv_in, 16 * C, wv_hi)
            queries_hi(0, 0)
            queries_dup(0, 0)
            for j in range(PAIRS):
                keys_hi(0, j)
                if j == 0:
                    queries_hi(0, 1)
                    queries_dup(0, 1)
            for i in range(PAIRS // 2):
                values_out(0, i, 0)
                if i == 1:
                    exps(0, 0)
                values_out(0, i, 1)
                if i in (1, 2):
                    values_in(1, i - 1)
            batch(0, False, True, True)
            with act.Fori(1, B - 2) as b:
                batch(b, True, True, True)
            batch(B - 2, True, True, False)
            batch(B - 1, True, False, False)

            def group(k, wt, g, routing=False):
                for m in range(M6):
                    if routing and m == 2:
                        act.wait_ge(route, 2)
                        act.activation(ex[:, :, :], lg[:, :, :], ACT.Exp).then_inc(route_exp, 1)
                    n = (k * G + g) * M6 + m
                    act.wait_ge(gate_mm, n + 1)
                    act.wait_ge(h_mul, n + 1)
                    act.activation(sl[0:MS[m], m % 2, :], gb[m % 2][0:MS[m], 0:GT], ACT.Silu
                                   ).then_inc(silu_done, 1)
                    if m == 2:
                        act.wait_ge(ffw_in, 64 * (k + 2))
                        act.wait_ge(down_mm, D0 + M6 * G * k)
                        weights_hi(1 - wt, piece(g))
                if k == 0:
                    act.wait_ge(down_mm, D0 + (k * G + g + 1) * M6)
                    for c in range(C):
                        act.activation(accT[:, c, bass.ds(g * GT, GT)], yb[c][:, 0:GT],
                                       ACT.Copy).then_inc(y_out, 1)

            def expert(k, wt):
                with act.Fori(0, G) as g:
                    group(k, wt, g)
                weights_hi(1 - wt, LAST)

            def last_expert(k):
                with act.Fori(0, G) as g:
                    for m in range(M6):
                        n = (k * G + g) * M6 + m
                        act.wait_ge(gate_mm, n + 1)
                        act.wait_ge(h_mul, n + 1)
                        act.activation(sl[0:MS[m], m % 2, :], gb[m % 2][0:MS[m], 0:GT], ACT.Silu
                                       ).then_inc(silu_done, 1)

            act.wait_ge(x1_done, X0 + B)
            with act.Fori(0, G // 2) as g:
                group(0, 0, g)
            residual_out(B - 1)
            group(0, 0, G // 2, True)
            for g in range(G // 2 + 1, G):
                group(0, 0, g)
            weights_hi(1, LAST)
            expert(1, 1)
            expert(2, 0)
            expert(3, 1)
            last_expert(4)

        @block.vector
        def _(dve):
            TILES = [(L, CT)] + [(SR, r) for r in range(CT)]

            def row_stats(t, part=(0, 1)):
                xt = x1[:, bass.ds(t, 1), :].rearrange("p a d -> p (a d)")
                if 0 in part:
                    dve.wait_ge(ctx_loaded, 16 * (t + 1))
                for n, r in [t for i in part for t in TILES[2 * i:2 * i + 2]]:
                    i = dve.bn_stats(st[0:n, r, :], ctx_raw[:, r, :] if r < CT else xt)
                if 1 not in part:
                    return
                i.then_inc(stats, 1)
                dve.wait_ge(stats, t + 1)
                plain(dve)
                for n, r in TILES:
                    i = dve.bn_aggr(mv[0:n, r, :], st[0:n, r, :])
                i.then_inc(aggr, 1)
                dve.wait_ge(aggr, t + 1)
                dve.tensor_scalar(ve[:, 0:CT], mv[:, 0:CT, 1], EPS, None, ALU.add)
                dve.tensor_scalar(ve[0:L, CT:CT + 1], mv[0:L, CT, 1:2], EPS, None, ALU.add
                                  ).then_inc(var_eps, 1)

            def row_norm(t, part):
                xt = x1[:, bass.ds(t, 1), :].rearrange("p a d -> p (a d)")
                if part == 0:
                    dve.wait_ge(rstd_done, t + 1)
                    if not (isinstance(t, int) and t == 0):
                        dve.wait_ge(kvt_done, 2 * t)
                for n, r in TILES[2 * part:2 * part + 2]:
                    dve.tensor_scalar(rows[0:n, r, :], ctx_raw[:, r, :] if r < CT else xt,
                                      mv[0:n, r, 0:1], rstd[0:n, r:r + 1],
                                      ALU.subtract, ALU.mult
                                      ).then_inc(lat_done if r == CT else ctx_norm, 1)
                if part == 1:
                    return
                dve.wait_ge(lat_done, t + 1)
                dve.bn_stats(lst[:, :], rows[0:L, CT, :]).then_inc(lstats, 1)
                dve.wait_ge(lstats, t + 1)
                plain(dve)
                dve.bn_aggr(lmv[:, :], lst[:, :]).then_inc(laggr, 1)
                dve.wait_ge(laggr, t + 1)
                dve.tensor_scalar(lve[:, :], lmv[:, 1:2], EPS, None, ALU.add
                                  ).then_inc(lvar_eps, 1)

            def latent_norm(t):
                dve.wait_ge(lrstd_done, t + 1)
                dve.tensor_scalar(rows[0:L, CT, :], rows[0:L, CT, :], lmv[:, 0:1], lrstd[:, 0:1],
                                  ALU.subtract, ALU.mult).then_inc(rows_done, 1)

            def split_lo(dst, full, hi, waits, done):
                for s, at_least in waits:
                    dve.wait_ge(s, at_least)
                dve.tensor_tensor(dst, full, SPLIT(hi), ALU.subtract).then_inc(done, 1)

            def values_in_hi(t):
                dve.wait_ge(val_done, 2 * t + 2)
                if not (isinstance(t, int) and t == 0):
                    dve.wait_ge(vproj, PAIRS * t)
                dve.tensor_copy(kv_h[:, :, :], val[:, :, :]).then_inc(kv_hi_done, 1)

            def values_in_lo(t):
                dve.wait_ge(kv_hi_done, t + 1)
                dve.tensor_tensor(kv_l[:, :, :], val[:, :, :], SPLIT(kv_h[:, :, :]),
                                  ALU.subtract).then_inc(kv_lo_done, 1)

            def keys_lo(t, j):
                for u in range(2):
                    dve.wait_ge(k_hi_done, H * t + 2 * j + u + 1)
                    i = dve.tensor_tensor(keys[HEAD[1 - u], j, u, :],
                                          key_bank(t, j)[HEAD[u], 0:KW],
                                          SPLIT(keys[HEAD[u], j, u, :]), ALU.subtract)
                i.then_inc(k_lo_done, 1)

            def queries_lo(t, half):
                dve.wait_ge(q_hi_done, 2 * t + half + 1)
                js = slice(4 * half, 4 * half + 4)
                for u in range(2):
                    i = dve.scalar_tensor_tensor(
                        q_l[HEAD[u], js, :],
                        bM[HEAD[u], 0:4 * L].rearrange("p (j l) -> p j l", j=4), DH ** -0.5,
                        SPLIT(q_h[HEAD[u], js, u, :]), ALU.mult, ALU.subtract)
                i.then_inc(q_lo_done, 1)

            def maxima(b, j):
                for u in range(2):
                    h = 2 * j + u
                    dve.wait_ge(scored, H * b + h + 1)
                    dve.tensor_reduce(nmax[:, h:h + 1], bS[u][0:L, 0:SK], AX.X, ALU.max,
                                      negate=True).then_inc(maxed, 1)

            def invert(b, h):
                dve.wait_ge(exped, S0 + H * b + h + 1)
                dve.reciprocal(rinv[:, h:h + 1], rsum[:, h:h + 1]).then_inc(inverted, 1)

            def turned_copy(b, j):
                dve.wait_ge(turned, T0 + H * b + 2 * j + 2)
                dve.wait_ge(pv_done, PAIRS * b + j + 1)
                dve.tensor_copy(probT[:, (2 * j + 1) % 4, :, :],
                                bT[1][0:KR, 0:KT * L].rearrange("p (s l) -> p s l", s=KT)
                                ).then_inc(turned_out[1], 1)

            def heads_lo(b, half):
                js = slice(4 * half, 4 * half + 4)
                split_lo(o_l[:, js, :], bO[:, 0:4 * L].rearrange("p (j l) -> p j l", j=4),
                         o_h[:, js, :], [(o_hi_done, 2 * b + half + 1)], o_lo_done)

            def rows_of(b):
                return x1[:, bass.ds(b, 1), :].rearrange("p a d -> p (a d)")

            def residual(b):
                dve.wait_ge(wo_done, W0 + b + 1)
                dve.scalar_tensor_tensor(rows_of(b), bM[0:L, 0:D], tgate[0:L, 0:1], rows_of(b),
                                         ALU.mult, ALU.add).then_inc(x1_done, 1)

            def residual_stats(b):
                dve.wait_ge(x1_done, X0 + b + 1)
                dve.bn_stats(fst[:, :], rows_of(b)).then_inc(fstats, 1)
                dve.wait_ge(fstats, b + 1)
                plain(dve)
                dve.bn_aggr(fmv[:, :], fst[:, :]).then_inc(faggr, 1)
                dve.wait_ge(faggr, b + 1)
                dve.tensor_scalar(fve[:, :], fmv[:, 1:2], EPS, None, ALU.add
                                  ).then_inc(fve_done, 1)

            def residual_norm(b):
                dve.wait_ge(frstd_done, b + 1)
                dve.wait_ge(ft_done, F0 + b)
                dve.tensor_scalar(frow[:, :], rows_of(b), fmv[:, 0:1], frstd[:, 0:1],
                                  ALU.subtract, ALU.mult).then_inc(frow_done, 1)

            def tokens_hi(g):
                tok = slice(g * GT, (g + 1) * GT)
                dve.tensor_copy(xn_h[:, :, tok], xnT[:, :, tok]).then_inc(xn_hi_done, 1)

            def weights_lo(count, parts):
                dve.wait_ge(ffw_hi, count)
                for n, cols in parts:
                    i = dve.tensor_tensor(w_l[0][0:n, cols], raw[0:n, cols],
                                          SPLIT(w_h[0][0:n, cols]), ALU.subtract)
                i.then_inc(ffw_lo, 1)

            def batch(b, before, next1, next2):
                for j in range(PAIRS):
                    if j > 0:
                        maxima(b, j)
                        turned_copy(b, j - 1)
                    if before and j == 0:
                        residual_stats(b - 1)
                    if before and j == 1:
                        residual_norm(b - 1)
                    if next2:
                        if j in (1, 2):
                            row_stats(b + 2, (j - 1,))
                        if j in (3, 5):
                            row_norm(b + 2, (j - 3) // 2)
                        if j == 5:
                            latent_norm(b + 2)
                    if next1 and j == 4:
                        queries_lo(b + 1, 0)
                    if j > 0:
                        invert(b, 2 * j)
                        invert(b, 2 * j + 1)
                    if not next1 and 2 <= j <= PIECES:
                        weights_lo(j - 1, piece(j - 2))
                    if next1:
                        keys_lo(b + 1, j)
                    if j == (4 if next1 else 5):
                        heads_lo(b, 0)
                if next1:
                    queries_lo(b + 1, 1)
                turned_copy(b, PAIRS - 1)
                heads_lo(b, 1)
                if not next1:
                    weights_lo(PIECES, LAST)
                    dve.wait_ge(scored, H * B)
                    dve.wait_ge(xnT_done, GB)
                    tokens_hi(0)
                if next2:
                    values_in_hi(b + 2)
                if next1:
                    maxima(b + 1, 0)
                    invert(b + 1, 0)
                    invert(b + 1, 1)
                residual(b)

            dve.wait_ge(x_in, 16)
            row_stats(0)
            row_norm(0, 0)
            row_norm(0, 1)
            latent_norm(0)
            for c in range(C):
                split_lo(wkv_l[:, c, 0:INNER], raw[:, c * INNER:(c + 1) * INNER],
                         wkv_h[:, c, 0:INNER], [(wk_hi, c + 1)], wk_lo)
            values_in_hi(0)
            values_in_lo(0)
            row_stats(1)
            queries_lo(0, 0)
            for j in range(PAIRS):
                keys_lo(0, j)
                if j == 0:
                    queries_lo(0, 1)
            row_norm(1, 0)
            row_norm(1, 1)
            maxima(0, 0)
            latent_norm(1)
            invert(0, 0)
            invert(0, 1)
            values_in_hi(1)
            values_in_lo(1)
            dve.wait_ge(x_rest_in, 16)
            dve.wait_ge(tanh_done, 1)
            batch(0, False, True, True)
            with dve.Fori(1, B - 2) as b:
                batch(b, True, True, True)
            batch(B - 2, True, True, False)
            batch(B - 1, True, False, False)

            residual_stats(B - 1)
            dve.wait_ge(xnT_done, (G - 1) * GB)
            for g in range(1, G - 1):
                tokens_hi(g)
            residual_norm(B - 1)

            def over_e(ap):
                return ap.unsqueeze(2).broadcast_to((L, B, E))

            scores = bank[3][0:L, 0:B * E].rearrange("p (b e) -> p b e", e=E)

            def before_each():
                for f in range(E):
                    def score_f(n):
                        return sc[:, :, f:f + 1].broadcast_to((L, B, n))
                    i = dve.tensor_tensor(beat[:, f, :, 0:f + 1], score_f(f + 1),
                                          sc[:, :, 0:f + 1], ALU.is_gt)
                    if f < E - 1:
                        i = dve.tensor_tensor(beat[:, f, :, f + 1:E], score_f(E - 1 - f),
                                              sc[:, :, f + 1:E], ALU.is_ge)
                return i

            def route_step(n):
                if n == 0:
                    dve.wait_ge(gated, 1)
                    i = dve.tensor_reduce(lmax[:, :], scores, AX.X, ALU.max)
                else:
                    dve.wait_ge(route, n)
                if n == 1:
                    i = dve.tensor_tensor(lg[:, :, :], scores, over_e(lmax[:, :]), ALU.subtract)
                if n == 2:
                    dve.wait_ge(route_exp, 1)
                    i = dve.tensor_reduce(esum[:, :], ex[:, :, :], AX.X, ALU.add)
                if n == 3:
                    i = dve.reciprocal(wsum[:, :], esum[:, :])
                if n == 4:
                    i = dve.tensor_tensor(sc[:, :, :], ex[:, :, :], over_e(wsum[:, :]), ALU.mult)
                if n == 5:
                    i = before_each()
                if n == 6:
                    i = dve.tensor_reduce(rank[:, :, :],
                                          beat[:, :, :, :].rearrange("p f b e -> p b e f"),
                                          AX.X, ALU.add)
                if n == 7:
                    i = dve.scalar_tensor_tensor(wsel[:, :, :], rank[:, :, :], 1.5, sc[:, :, :],
                                                 ALU.is_lt, ALU.mult)
                if n == 8:
                    i = dve.tensor_reduce(esum[:, :], wsel[:, :, :], AX.X, ALU.add)
                if n == 9:
                    i = dve.tensor_scalar(esum[:, :], esum[:, :], 1e-20, None, ALU.add)
                if n == 10:
                    i = dve.reciprocal(wsum[:, :], esum[:, :])
                if n == 11:
                    i = dve.tensor_tensor(comb[:, :, :].rearrange("p e b -> p b e"),
                                          wsel[:, :, :], over_e(wsum[:, :]), ALU.mult)
                i.then_inc(route, 1)

            def group(k, wt, g, steps=()):
                for m in range(M6):
                    n = (k * G + g) * M6 + m
                    dve.wait_ge(silu_done, n + 1)
                    dve.wait_ge(up_mm, n + 1)
                    dve.wait_ge(h_lo_done, n + 1)
                    dve.tensor_tensor(hf[0:MS[m], m % 2, :], ub[m % 2][0:MS[m], 0:GT],
                                      sl[0:MS[m], m % 2, :], ALU.mult).then_inc(h_mul, 1)
                    dve.wait_ge(h_mul, H0 + n + 1)
                    dve.wait_ge(down_mm, D0 + M6 * (k * G + g))
                    dve.tensor_copy(h_h[0:MS[m], m, :], hf[0:MS[m], m % 2, :]
                                    ).then_inc(h_hi_done, 1)
                    split_lo(h_l[0:MS[m], m, :], hf[0:MS[m], m % 2, :], h_h[0:MS[m], m, :],
                             [(h_hi_done, n + 1)], h_lo_done)
                    for step in steps[2 * m:2 * m + 2]:
                        route_step(step)

            def weighted(k, wt, g, turn):
                dve.wait_ge(cb_in[wt], 16 * turn)
                dve.wait_ge(down_mm, D0 + (k * G + g + 1) * M6)
                dve.wait_ge(acc_done, A0 + C * ((k - 1) * G + g))
                for c in range(C):
                    dve.tensor_tensor(ytmp[:, c, :], yb[c][:, 0:GT],
                                      cb[wt][:, bass.ds(g * GT, GT)], ALU.mult
                                      ).then_inc(y_out, 1)

            def expert(k, wt, turn):
                with dve.Fori(0, G) as g:
                    group(k, wt, g)
                    weighted(k, wt, g, turn)

            with dve.Fori(0, G // 2) as g:
                group(0, 0, g)
            dve.wait_ge(xnT_done, B)
            tokens_hi(G - 1)
            group(0, 0, G // 2, range(2))
            group(0, 0, G // 2 + 1, range(2, ROUTED))
            dve.wait_ge(comb_t, 1)
            dve.tensor_copy(combT[:, :], bM[0:E * B, 0:L]).then_inc(comb_c, 1)
            with dve.Fori(0, E // 2) as i:
                expert(2 * i + 1, 1, i + 1)
                expert(2 * i + 2, 0, i + 1)

            with dve.Fori(0, B // 2) as i:
                for u in range(2):
                    b = 2 * i + u
                    dve.wait_ge(yt_done, b + 1)
                    dve.scalar_tensor_tensor(rows_of(b), rb[u][0:L, 0:D], tgate[0:L, 1:2],
                                             rows_of(b), ALU.mult, ALU.add).then_inc(fin, 1)

        @block.gpsimd
        def _(pool):
            pool.memset(ident[:, :], 0.0).then_inc(ident0, 1)
            pool.memset(neghalf[:, :], -0.5).then_inc(const_set, 1)
            pool.memset(val[:, :, SK:KW], 0.0).then_inc(const_set, 1)
            pool.memset(prob[:, :, SK:KW], 0.0).then_inc(const_set, 1)
            pool.wait_ge(ident0, 1)
            pool.affine_select(out=ident[:, :], in_=ident[:, :], compare_op=ALU.not_equal,
                               fill=1.0, base=0, pattern=[[-1, P]], channel_multiplier=1
                               ).then_inc(const_set, 1)
            for s, start in ((exped, S0), (turned, T0), (pv_done, V0),
                             (turned_out[0], C0), (turned_out[1], C0),
                             (o_lo_done, O0), (x1_done, X0), (wo_done, W0), (ft_done, F0),
                             (h_mul, H0), (h_lo_done, H0),
                             (down_mm, D0), (y_out, Y0), (acc_done, A0)):
                pool.sem_inc(s, start)
            pool.wait_ge(const_set, 4)

            def power(dst, src, cols):
                return pool.tensor_tensor(dst, src, cols, ALU.pow)

            def row_rstd(t):
                pool.wait_ge(var_eps, t + 1)
                power(rstd[:, 0:CT], ve[:, 0:CT], neghalf[0:SR, 0:CT])
                power(rstd[0:L, CT:CT + 1], ve[0:L, CT:CT + 1], neghalf[0:L, 0:1]
                      ).then_inc(rstd_done, 1)

            def latent_rstd(t):
                pool.wait_ge(lvar_eps, t + 1)
                power(lrstd[:, :], lve[:, :], neghalf[0:L, 0:1]).then_inc(lrstd_done, 1)

            def normalise(b, j):
                for u in range(2):
                    h = 2 * j + u
                    pool.wait_ge(inverted, H * b + h + 1)
                    plain(pool)
                    pool.tensor_scalar(prob[:, h % 4, 0:SK], prob[:, h % 4, 0:SK],
                                       rinv[:, h:h + 1], 1.0, ALU.mult, ALU.mult
                                       ).then_inc(normed, 1)

            def queries_in(t):
                pool.wait_ge(val_done, 2 * t + 2)
                if not (isinstance(t, int) and t == 0):
                    pool.wait_ge(qproj, 2 * t)
                    plain(pool)
                pool.tensor_copy(xq[:, :, :], val[:, :, S:SK]).then_inc(xq_done, 1)

            def values_in_lo(t):
                pool.wait_ge(kv_hi_done, t + 1)
                pool.tensor_tensor(kv_l[:, :, :], val[:, :, :], SPLIT(kv_h[:, :, :]),
                                   ALU.subtract).then_inc(kv_lo_done, 1)

            def residual_rstd(b):
                pool.wait_ge(fve_done, b + 1)
                power(frstd[:, :], fve[:, :], neghalf[0:L, 0:1]).then_inc(frstd_done, 1)

            def weights_lo(wt, count, parts):
                pool.wait_ge(ffw_hi, count)
                for n, cols in parts:
                    i = pool.tensor_tensor(w_l[wt][0:n, cols], raw[0:n, cols],
                                           SPLIT(w_h[wt][0:n, cols]), ALU.subtract)
                i.then_inc(ffw_lo, 1)

            def tokens_lo(g):
                tok = slice(g * GT, (g + 1) * GT)
                pool.wait_ge(xn_hi_done, g + 1)
                pool.tensor_tensor(xn_l[:, :, tok], xnT[:, :, tok], SPLIT(xn_h[:, :, tok]),
                                   ALU.subtract).then_inc(xn_lo_done, 1)

            def project_out_lo(n):
                pool.wait_ge(wo_hi, n + 1)
                js = slice(HP * n, HP * (n + 1))
                pool.tensor_tensor(wo_l[:, js, :], wo_raw(n), SPLIT(wo_h[:, js, :]), ALU.subtract
                                   ).then_inc(wo_lo, 1)

            def batch(b, before, next1, next2):
                for j in range(PAIRS):
                    if before and j == 1:
                        residual_rstd(b - 1)
                    if j > 0:
                        normalise(b, j)
                    if isinstance(b, int) and b == 0 and j in (2, 3):
                        project_out_lo(j - 2)
                    if next2 and j == 2:
                        row_rstd(b + 2)
                    if next2 and j == 3:
                        latent_rstd(b + 2)
                if next2:
                    values_in_lo(b + 2)
                    queries_in(b + 2)
                if next1:
                    normalise(b + 1, 0)

            row_rstd(0)
            latent_rstd(0)
            queries_in(0)
            row_rstd(1)
            for c in range(C):
                pool.wait_ge(wv_hi, c + 1)
                pool.tensor_tensor(wkv_l[:, c, INNER:2 * INNER],
                                   raw[:, (C + c) * INNER:(C + c + 1) * INNER],
                                   SPLIT(wkv_h[:, c, INNER:2 * INNER]), ALU.subtract
                                   ).then_inc(wv_lo, 1)
            latent_rstd(1)
            normalise(0, 0)
            queries_in(1)
            batch(0, False, True, True)
            with pool.Fori(1, B - 2) as b:
                batch(b, True, True, True)
            batch(B - 2, True, True, False)
            batch(B - 1, True, False, False)

            tokens_lo(0)
            residual_rstd(B - 1)
            for g in range(1, G - 1):
                tokens_lo(g)

            def added(k, g):
                for c in range(C):
                    acc = accT[:, c, bass.ds(g * GT, GT)]
                    pool.wait_ge(y_out, Y0 + C * (k * G + g) + c + 1)
                    pool.tensor_tensor(acc, acc, ytmp[:, c, :], ALU.add).then_inc(acc_done, 1)

            def expert(k, wt):
                with pool.Fori(0, G) as g:
                    weights_lo(1 - wt, PIECES * (k + 1) + g + 1, piece(g))
                    added(k, g)
                weights_lo(1 - wt, PIECES * (k + 2), LAST)

            with pool.Fori(0, G - 1) as g:
                weights_lo(1, PIECES + g + 1, piece(g))
            tokens_lo(G - 1)
            weights_lo(1, 2 * PIECES - 1, piece(G - 1))
            weights_lo(1, 2 * PIECES, LAST)
            expert(1, 1)
            expert(2, 0)
            expert(3, 1)
            with pool.Fori(0, G) as g:
                added(E, g)


def kernel(x, ctx_1024, g_xattn, g_ffn, L0_xattn_Wq, L0_xattn_Wkv, L0_xattn_Wo, L0_xattn_ln1_w,
           L0_xattn_ln1_b, L0_xattn_ln2_w, L0_xattn_ln2_b, L0_ffn_gate_w, L0_ffn_eg, L0_ffn_eu,
           L0_ffn_ed, L0_ffn_sg, L0_ffn_su, L0_ffn_sd):
    import numpy as np
    import concourse.bacc as bacc
    from concourse.bass_utils import run_bass_kernel_spmd

    def experts(shared, routed):
        both = np.concatenate([np.asarray(shared)[None], np.asarray(routed)])
        return both.transpose(0, 2, 1)

    ln_wb = np.stack([np.asarray(a).reshape(-1, P) for a in (
        L0_xattn_ln1_w, L0_xattn_ln1_b, L0_xattn_ln2_w, L0_xattn_ln2_b)]).transpose(2, 0, 1)

    ins = [("x", x), ("ctx", ctx_1024), ("g_xattn", g_xattn), ("g_ffn", g_ffn),
           ("wq", L0_xattn_Wq), ("wkv", L0_xattn_Wkv), ("wo", L0_xattn_Wo),
           ("ln_wb", ln_wb),
           ("gate_wT", np.asarray(L0_ffn_gate_w).T),
           ("gateT", experts(L0_ffn_sg, L0_ffn_eg)), ("upT", experts(L0_ffn_su, L0_ffn_eu)),
           ("downT", experts(L0_ffn_sd, L0_ffn_ed))]
    nc = bacc.Bacc("TRN2", target_bir_lowering=False, num_devices=1)
    arrays, aps = {}, []
    for name, a in ins:
        a = np.ascontiguousarray(a)
        arrays[f"in_{name}"] = a
        aps.append(nc.dram_tensor(f"in_{name}", a.shape, mybir.dt.from_np(a.dtype),
                                  kind="ExternalInput").ap())
    shape = np.asarray(x).shape
    out = nc.dram_tensor("out_x", shape, F32, kind="ExternalOutput").ap()
    flamingo_block(nc, *aps, out)
    r = run_bass_kernel_spmd(nc, [arrays], core_ids=[0])
    return r.results[0]["out_x"]
```

```python
from contextlib import ExitStack

import concourse.bass as bass
from concourse import mybir

ALU = mybir.AluOpType
ACT = mybir.ActivationFunctionType
AX = mybir.AxisListType
F32 = mybir.dt.float32
F32R = mybir.dt.float32r

EPS = 1e-5
P = 128
DH = 64
KT = 4
CT = 3
PAIRS = 8
GB = 4


def flamingo_block(nc, x, ctx_in, g_xattn, g_ffn, Wq, Wkv, Wo, ln_wb,
                   gate_wT, gate_upT, downT, out):
    B, L, D = x.shape
    S = ctx_in.shape[1]
    INNER = Wq.shape[1]
    E1, I, _ = downT.shape
    E = E1 - 1
    C = D // P
    SK = S + L
    KW = (SK + KT - 1) // KT * KT
    KR = KW // KT
    SR = S // CT
    H = INNER // DH
    assert H == 2 * PAIRS and S % CT == 0 and KW - SK == 1 and C == 2
    N = B * L
    GT = GB * L
    G = B // GB
    MT = I // P
    REST = I - MT * P
    M6 = MT + 1
    assert MT == 5 and 0 < REST <= 64 and 2 * M6 == B - GB
    MR = MT - 1
    ROWS = [slice(0, P)] * MR + [slice(64, 64 + REST), slice(0, P)]
    FROM = [m * P for m in range(MR)] + [MT * P, MR * P]
    GU = 2 * MT * P + 64 + REST
    assert gate_upT.shape[2] == GU
    GUW = C * GU
    GQ = GUW // G
    FW = GUW + M6 * D
    SPLIT = lambda t: t.bitcast(F32)

    with ExitStack() as life:
        def sem(name):
            return life.enter_context(nc.semaphore(name))

        def sb(stack, name, shape, dt=F32):
            return stack.enter_context(nc.sbuf_tensor(name, shape, dt))

        x1 = sb(life, "x1", [L, B, D])
        raw = sb(life, "raw", [P, FW])
        ident = sb(life, "ident", [P, P])
        gates = sb(life, "gates", [P, 2])
        tgate = sb(life, "tgate", [P, 2])
        gw = sb(life, "gw", [P, C, E])
        neghalf = sb(life, "neghalf", [P, CT])
        fst = sb(life, "fst", [L, 6])
        fmv = sb(life, "fmv", [L, 2])
        fve = sb(life, "fve", [L, 1])
        frstd = sb(life, "frstd", [L, 1])
        frow = sb(life, "frow", [L, D])
        xnT = sb(life, "xnT", [P, C, N])
        cb = [xnT[:, i, :] for i in range(2)]

        one = ExitStack()
        wkv_h = sb(one, "wkv_h", [P, C, 2 * INNER], F32R)
        wkv_l = sb(one, "wkv_l", [P, C, 2 * INNER], F32R)
        wq = sb(one, "wq", [P, C, INNER])
        lnw = sb(one, "lnw", [P, 4, C])
        ctx_raw = sb(one, "ctx_raw", [SR, CT, D])
        rows = sb(one, "rows", [SR, CT + 1, D])
        st = sb(one, "st", [SR, CT + 1, 6])
        mv = sb(one, "mv", [SR, CT + 1, 2])
        ve = sb(one, "ve", [SR, CT + 1])
        rstd = sb(one, "rstd", [SR, CT + 1])
        lst = sb(one, "lst", [L, 6])
        lmv = sb(one, "lmv", [L, 2])
        lve = sb(one, "lve", [L, 1])
        lrstd = sb(one, "lrstd", [L, 1])
        val = sb(one, "val", [P, C, KW])
        kv_h = sb(one, "kv_h", [P, C, KW], F32R)
        kv_l = sb(one, "kv_l", [P, C, KW], F32R)
        xq = sb(one, "xq", [P, C, L])
        keys = sb(one, "keys", [P, PAIRS, 2, KW], F32R)
        wo_h = sb(one, "wo_h", [P, PAIRS, D], F32R)
        wo_l = sb(one, "wo_l", [P, PAIRS, D], F32R)
        q_h = sb(one, "q_h", [P, PAIRS, 2, L], F32R)
        q_l = sb(one, "q_l", [P, PAIRS, L], F32R)
        v = sb(one, "v", [KR, KT, INNER])
        nmax = sb(one, "nmax", [L, H])
        rsum = sb(one, "rsum", [L, H])
        rinv = sb(one, "rinv", [L, H])
        prob = sb(one, "prob", [L, 4, KW])
        probT = sb(one, "probT", [KR, 4, KT, L])
        o_h = sb(one, "o_h", [P, PAIRS, L], F32R)
        o_l = sb(one, "o_l", [P, PAIRS, L], F32R)
        one.close()

        two = ExitStack()
        w_h0 = sb(two, "w_h0", [P, FW], F32R)
        w_l0 = sb(two, "w_l0", [P, FW], F32R)
        xn_h = sb(two, "xn_h", [P, C, N], F32R)
        xn_l = sb(two, "xn_l", [P, C, N], F32R)
        w_h = [w_h0, sb(two, "w_h1", [P, FW], F32R)]
        w_l = [w_l0, sb(two, "w_l1", [P, FW], F32R)]
        accT = sb(two, "accT", [P, C, N])
        lg = sb(two, "lg", [L, B, E])
        lmax = sb(two, "lmax", [L, B])
        ex = sb(two, "ex", [L, B, E])
        esum = sb(two, "esum", [L, B])
        sc = sb(two, "sc", [L, B, E])
        beat = sb(two, "beat", [L, E, B, E])
        rank = sb(two, "rank", [L, B, E])
        wsel = sb(two, "wsel", [L, B, E])
        wsum = sb(two, "wsum", [L, B])
        comb = sb(two, "comb", [L, E, B])
        combT = sb(two, "combT", [E * B, L])
        sl = sb(two, "sl", [P, 2, GT])
        hf = sb(two, "hf", [P, 2, GT])
        h_h = sb(two, "h_h", [P, M6, GT], F32R)
        h_l = sb(two, "h_l", [P, M6, GT], F32R)
        ytmp = sb(two, "ytmp", [P, C, GT])
        two.close()
        comb_dram = nc.dram_tensor("comb_dram", (E * B, L), F32, kind="Internal").ap()

        bank = [life.enter_context(nc.psum_tensor(f"bank{i}", [P, 512], F32)) for i in range(8)]
        bS = bank[0:2]
        bT = bank[2:4]
        bK, bV, bO, bM = bank[4:8]
        gb, ub, yb = bank[0:2], bank[4:6], [bank[6], bank[2]]
        rb = [bank[3], bank[7]]

        x_in, x_rest_in, ctx_loaded, small_in, wq_in, out_done = map(sem, (
            "x_in", "x_rest_in", "ctx_loaded", "small_in", "wq_in", "out_done"))
        wk_in, wv_in, wo_in = map(sem, ("wk_in", "wv_in", "wo_in"))
        wk_hi, wk_lo, wv_hi, wv_lo, wo_hi, wo_lo = map(sem, (
            "wk_hi", "wk_lo", "wv_hi", "wv_lo", "wo_hi", "wo_lo"))
        ident0, const_set, tanh_done = map(sem, ("ident0", "const_set", "tanh_done"))
        stats, aggr, var_eps, rstd_done, lat_done, ctx_norm = map(sem, (
            "stats", "aggr", "var_eps", "rstd_done", "lat_done", "ctx_norm"))
        lstats, laggr, lvar_eps, lrstd_done, rows_done = map(sem, (
            "lstats", "laggr", "lvar_eps", "lrstd_done", "rows_done"))
        kvt_done, val_done, kv_hi_done, kv_lo_done, xq_done = map(sem, (
            "kvt_done", "val_done", "kv_hi_done", "kv_lo_done", "xq_done"))
        kproj, k_hi_done, k_lo_done, vproj, v_out, qproj, q_hi_done, q_lo_done = map(sem, (
            "kproj", "k_hi_done", "k_lo_done", "vproj", "v_out", "qproj", "q_hi_done", "q_lo_done"))
        scored, maxed, exped, inverted, normed, turned, q_dup_done = map(sem, (
            "scored", "maxed", "exped", "inverted", "normed", "turned", "q_dup_done"))
        turned_out = [sem(f"turned_out{u}") for u in range(2)]
        pv_done, o_hi_done, o_lo_done, wo_done, x1_done = map(sem, (
            "pv_done", "o_hi_done", "o_lo_done", "wo_done", "x1_done"))
        fstats, faggr, fve_done, frstd_done, frow_done, ft_done, xnT_done = map(sem, (
            "fstats", "faggr", "fve_done", "frstd_done", "frow_done", "ft_done", "xnT_done"))
        xn_hi_done, xn_lo_done, gated = map(sem, ("xn_hi_done", "xn_lo_done", "gated"))
        route, route_exp, comb_t, comb_c, comb_out = map(sem, (
            "route", "route_exp", "comb_t", "comb_c", "comb_out"))
        cb_in = [sem(f"cb_in{i}") for i in range(2)]
        ffw_in, ffw_hi, ffw_lo, gw_in = map(sem, ("ffw_in", "ffw_hi", "ffw_lo", "gw_in"))
        gate_mm, up_mm, silu_done, h_mul, h_hi_done, h_lo_done, down_mm, y_out, acc_done = map(sem, (
            "gate_mm", "up_mm", "silu_done", "h_mul", "h_hi_done", "h_lo_done", "down_mm", "y_out",
            "acc_done"))
        yt_done, fin, waited = map(sem, ("yt_done", "fin", "waited"))

        S0 = 1
        T0 = 3
        C0 = 1
        V0 = 2
        O0 = 1
        X0 = 1
        W0 = 1
        F0 = 1
        H0 = 2
        D0 = 1
        Y0 = 1
        A0 = 1

        ROUTED = 12

        def piece(g):
            return (ROWS[0], bass.ds(g * GQ, GQ)), (ROWS[0], bass.ds(g * D + GUW, D))
        LAST = [((ROWS[m], slice(GUW + m * D, GUW + (m + 1) * D)),) for m in (MT, MR)]
        PIECES = 6

        def plain(eng):
            eng.sem_inc(waited, 1)

        def value_bank(t, n):
            return bK if n == PAIRS - 1 or isinstance(t, int) and t == 0 and n % 2 else bV

        def key_bank(t, j):
            return bV if j == 0 or isinstance(t, int) and t == 0 and j % 2 == 0 else bK

        def score_banks(b, j):
            last = isinstance(b, int) and b == B - 1
            return bank[4:6] if last and j % 2 else bS

        def heads_bank(b, half):
            return bM if isinstance(b, int) and b == B - 1 and half else bO

        HP = PAIRS // 2

        def wo_raw(n):
            return raw[:, n * HP * D:(n + 1) * HP * D].rearrange("p (j d) -> p j d", j=HP)

        HEAD = [slice(DH * u, DH * (u + 1)) for u in range(2)]

        block = life.enter_context(nc.Block())

        @block.sync
        def _(sp):
            def load_ctx(t):
                if not (isinstance(t, int) and t == 0):
                    sp.wait_ge(ctx_norm, CT * t)
                sp.dma_start(ctx_raw[:, :, :],
                             ctx_in[bass.ds(t, 1), :, :].rearrange("a (c p) d -> p (a c) d", p=SR)
                             ).then_inc(ctx_loaded, 16)

            load_ctx(0)
            sp.dma_start(x1[:, 0:2, :], x[0:2, :, :].rearrange("b l d -> l b d")
                         ).then_inc(x_in, 16)
            sp.dma_start(lnw[:, :, :], ln_wb).then_inc(small_in, 16)
            sp.dma_start(gates[:, 0:1], g_xattn.rearrange("(a n) -> a n", a=1).broadcast_to((P, 1))
                         ).then_inc(small_in, 16)
            sp.dma_start(gates[:, 1:2], g_ffn.rearrange("(a n) -> a n", a=1).broadcast_to((P, 1))
                         ).then_inc(small_in, 16)
            for c in range(C):
                sp.dma_start(raw[:, c * INNER:(c + 1) * INNER],
                             Wkv[c * P:(c + 1) * P, 0:INNER]).then_inc(wk_in, 16)
            sp.dma_start(wq[:, :, :], Wq.rearrange("(c p) n -> p c n", p=P)).then_inc(wq_in, 16)
            for c in range(C):
                sp.dma_start(raw[:, (C + c) * INNER:(C + c + 1) * INNER],
                             Wkv[c * P:(c + 1) * P, INNER:2 * INNER]).then_inc(wv_in, 16)
            load_ctx(1)
            sp.wait_ge(wk_lo, C)
            sp.dma_start(raw[:, 0:PAIRS * D].rearrange("p (j d) -> p j d", j=PAIRS),
                         Wo.rearrange("(j p) d -> p j d", p=P)).then_inc(wo_in, 16)
            sp.dma_start(gw[:, :, :], gate_wT.rearrange("(c p) e -> p c e", p=P)
                         ).then_inc(gw_in, 16)
            sp.dma_start(x1[:, 2:B, :], x[2:B, :, :].rearrange("b l d -> l b d")
                         ).then_inc(x_rest_in, 16)
            with sp.Fori(2, B) as t:
                load_ctx(t)

            def load_expert(k):
                sp.dma_start(raw[:, 0:GUW].rearrange("p (c i) -> p c i", c=C),
                             gate_upT[k, :, :].rearrange("(c p) i -> p c i", p=P)
                             ).then_inc(ffw_in, 16)
                sp.dma_start(
                    raw[:, GUW:GUW + MR * D].rearrange("p (m d) -> p m d", d=D),
                    downT[k, 0:MR * P, :].rearrange("(m p) d -> p m d", p=P)).then_inc(ffw_in, 16)
                for m in (MR, MT):
                    n = ROWS[m].stop - ROWS[m].start
                    sp.dma_start(raw[ROWS[m], GUW + m * D:GUW + (m + 1) * D],
                                 downT[k, FROM[m]:FROM[m] + n, :]).then_inc(ffw_in, 16)

            def load_comb(k):
                sp.dma_start(cb[k % 2][:, :],
                             comb_dram[(k - 1) * B:k * B, :].rearrange("b l -> (b l)")
                             .partition_broadcast(P)).then_inc(cb_in[k % 2], 16)

            sp.wait_ge(wv_lo, C)
            sp.wait_ge(wo_lo, 2)
            load_expert(0)
            sp.wait_ge(ffw_lo, PIECES)
            load_expert(1)
            sp.wait_ge(comb_c, 1)
            sp.dma_start(comb_dram, combT[:, :]).then_inc(comb_out, 16)
            sp.wait_ge(comb_out, 16)
            sp.wait_ge(xn_lo_done, G)
            load_comb(1)
            load_comb(2)
            for k in range(2, E1):
                sp.wait_ge(ffw_lo, PIECES * k)
                load_expert(k)
                if k >= 3:
                    sp.wait_ge(y_out, Y0 + C * G * (k - 1))
                    load_comb(k)
            QB = B // 4
            for q in range(4):
                sp.wait_ge(fin, QB * (q + 1))
                sp.dma_start(out[q * QB:(q + 1) * QB, :, :].rearrange("b l d -> l b d"),
                             x1[:, q * QB:(q + 1) * QB, :]).then_inc(out_done, 16)
            sp.wait_ge(out_done, 64)

        @block.tensor
        def _(pe):
            def three(out_ap, w_hi, w_lo, m_hi, m_lo, start, stop, after=lambda n: None):
                pe.matmul(out_ap, w_hi, m_hi, start=start, stop=False)
                after(0)
                pe.matmul(out_ap, w_hi, m_lo, start=False, stop=False)
                after(1)
                mm = pe.matmul(out_ap, w_lo, m_hi, start=False, stop=stop)
                after(2)
                return mm

            def turn_rows(t, c, bank_free):
                pe.wait_ge(rows_done, t + 1)
                for s, at_least in bank_free:
                    pe.wait_ge(s, at_least)
                for r in range(CT + 1):
                    n = SR if r < CT else L
                    mm = pe.transpose(bM[:, r * SR:r * SR + n], rows[0:n, r, c * P:(c + 1) * P],
                                      ident[0:n, 0:n])
                mm.then_inc(kvt_done, 1)

            def project_q(t, half, bank_free):
                pe.wait_ge(xq_done, t + 1)
                for s, at_least in bank_free:
                    pe.wait_ge(s, at_least)
                for i in range(4):
                    j = 4 * half + i
                    for c in range(C):
                        mm = pe.matmul(bM[:, i * L:(i + 1) * L], wq[:, c, j * P:(j + 1) * P],
                                       xq[:, c, :], start=(c == 0), stop=(c == C - 1))
                mm.then_inc(qproj, 1)

            def project_k(t, j):
                if j == 0:
                    pe.wait_ge(kv_lo_done, t + 1)
                    if not (isinstance(t, int) and t == 0):
                        pe.wait_ge(v_out, PAIRS * t - 1)
                elif j == 1:
                    if not (isinstance(t, int) and t == 0):
                        pe.wait_ge(v_out, PAIRS * t)
                elif not (isinstance(t, int) and t == 0):
                    pe.wait_ge(k_lo_done, PAIRS * t + j)
                else:
                    pe.wait_ge(k_lo_done, j - 1)
                for c in range(C):
                    mm = three(key_bank(t, j)[:, 0:KW], wkv_h[:, c, j * P:(j + 1) * P],
                               wkv_l[:, c, j * P:(j + 1) * P], kv_h[:, c, :], kv_l[:, c, :],
                               c == 0, c == C - 1)
                mm.then_inc(kproj, 1)

            def project_v(t, i, half):
                part = 2 * i + half
                to = value_bank(t, part)
                if isinstance(t, int) and t == 0:
                    if part < 2:
                        pe.wait_ge(k_lo_done, PAIRS - 1 + part)
                    else:
                        pe.wait_ge(v_out, part - 1)
                elif part == PAIRS - 1:
                    pe.wait_ge(k_lo_done, PAIRS * (t + 1))
                elif part > 0:
                    pe.wait_ge(v_out, PAIRS * t + part)
                for n in range(2):
                    for c in range(C):
                        s = 2 * half + n
                        cols = slice(INNER + 2 * P * i, INNER + 2 * P * (i + 1))
                        keys = slice(s * KR, (s + 1) * KR)
                        mm = three(to[0:KR, n * 2 * P:(n + 1) * 2 * P], kv_h[:, c, keys],
                                   kv_l[:, c, keys], wkv_h[:, c, cols], wkv_l[:, c, cols],
                                   c == 0, c == C - 1)
                mm.then_inc(vproj, 1)

            def scores(b, j):
                pe.wait_ge(k_lo_done, PAIRS * b + j + 1)
                pe.wait_ge(q_lo_done, 2 * b + j // 4 + 1)
                pe.wait_ge(q_dup_done, 2 * b + j // 4 + 1)
                bS = score_banks(b, j)
                last = isinstance(b, int) and b == B - 1
                if last and j == 1:
                    pe.wait_ge(v_out, PAIRS * B)
                for u in range(2):
                    pe.wait_ge(exped, H * b + 2 * j + u - (2 if last else 0))
                    pe.matmul(bS[u][0:L, 0:KW], q_h[:, j, u, :], keys[:, j, u, :],
                              start=True, stop=False)
                for u in range(2):
                    pe.matmul(bS[u][0:L, 0:KW], q_l[HEAD[u], j, :], keys[HEAD[u], j, u, :],
                              start=False, stop=True).then_inc(scored, 1)

            def turn(b, j):
                for u in range(2):
                    n = H * b + 2 * j + u
                    pe.wait_ge(normed, n + 1)
                    pe.wait_ge(turned_out[u], PAIRS * b + j + 1)
                    for s in range(KT):
                        mm = pe.transpose(bT[u][0:KR, s * L:(s + 1) * L],
                                          prob[:, (2 * j + u) % 4, s * KR:(s + 1) * KR],
                                          ident[0:L, 0:L])
                    mm.then_inc(turned, 1)

            def weigh(b, j):
                for u in range(2):
                    pe.wait_ge(turned_out[u], C0 + PAIRS * b + j + 1)
                if j % 2 == 0:
                    pe.wait_ge(v_out, PAIRS * b + j + 2)
                bO = heads_bank(b, j // 4)
                if j % 4 == 0:
                    if bO is bM:
                        pe.wait_ge(xnT_done, B - 1)
                    else:
                        pe.wait_ge(o_lo_done, O0 + 2 * b + j // 4)
                for s in range(KT):
                    for u in range(2):
                        mm = pe.matmul(bO[DH * u:DH * (u + 1), (j % 4) * L:(j % 4 + 1) * L],
                                       v[:, s, P * j + DH * u:P * j + DH * (u + 1)],
                                       probT[:, (2 * j + u) % 4, s, :],
                                       start=(s == 0), stop=(s == KT - 1))
                mm.then_inc(pv_done, 1)

            def project_out(b, bank_free):
                if isinstance(b, int) and b == 0:
                    pe.wait_ge(wo_lo, 2)
                pe.wait_ge(o_lo_done, O0 + 2 * b + 2)
                for s, at_least in bank_free:
                    pe.wait_ge(s, at_least)
                for j in range(PAIRS):
                    mm = three(bM[0:L, 0:D], o_h[:, j, :], o_l[:, j, :], wo_h[:, j, :],
                               wo_l[:, j, :], j == 0, j == PAIRS - 1)
                mm.then_inc(wo_done, 1)

            def turn_ffn(b, bank_free):
                pe.wait_ge(frow_done, b + 1)
                for s, at_least in bank_free:
                    pe.wait_ge(s, at_least)
                for c in range(C):
                    mm = pe.transpose(bM[:, c * L:(c + 1) * L], frow[:, c * P:(c + 1) * P],
                                      ident[0:L, 0:L])
                mm.then_inc(ft_done, 1)

            def batch(b, before, next1, next2):
                for j in range(PAIRS):
                    if j > 0:
                        scores(b, j)
                        if not next1 and j > 1:
                            weigh(b, j - 2)
                        turn(b, j - 1)
                    if next1:
                        project_k(b + 1, j)
                        if j >= 2:
                            project_v(b + 1, (j - 2) // 2, j % 2)
                    if next1 and j == 1:
                        project_q(b + 1, 0, [(x1_done, X0 + b)])
                    if next1 and j == PAIRS - 1:
                        project_q(b + 1, 1, [(val_done, 2 * b + 6)] if next2
                                  else [(xnT_done, b)])
                    if j > 0 and next1:
                        weigh(b, j - 1)
                    if before and j == 4:
                        turn_ffn(b - 1, [(q_lo_done, 2 * b + 3)] if next1 else [])
                    if next2 and j == 5:
                        turn_rows(b + 2, 0, [(xnT_done, b)] if before else [(q_lo_done, 2 * b + 3)])
                    if next2 and j == 6:
                        turn_rows(b + 2, 1, [(val_done, 2 * b + 5)])
                if not next1:
                    weigh(b, PAIRS - 2)
                turn(b, PAIRS - 1)
                if next1:
                    project_v(b + 1, 3, 0)
                weigh(b, PAIRS - 1)
                if next1:
                    project_v(b + 1, 3, 1)
                    scores(b + 1, 0)
                    project_out(b, [(q_lo_done, 2 * b + 4)])

            pe.wait_ge(const_set, 4)
            turn_rows(0, 0, [])
            turn_rows(0, 1, [(val_done, 1)])
            pe.wait_ge(wq_in, 16)
            project_q(0, 0, [(val_done, 2)])
            pe.wait_ge(wk_lo, C)
            for j in range(PAIRS):
                project_k(0, j)
                if j == 0:
                    project_q(0, 1, [(q_lo_done, 1)])
            pe.wait_ge(wv_lo, C)
            for i in range(PAIRS // 2):
                project_v(0, i, 0)
                if i == 0:
                    scores(0, 0)
                project_v(0, i, 1)
                if i == 1:
                    turn_rows(1, 0, [(q_lo_done, 2)])
                if i == 2:
                    turn_rows(1, 1, [(val_done, 3)])
            batch(0, False, True, True)
            with pe.Fori(1, B - 2) as b:
                batch(b, True, True, True)
            batch(B - 2, True, True, False)
            batch(B - 1, True, False, False)

            def routing_product(i):
                b, c = i // 2, i % 2
                if i < C * B:
                    if i == C * (B - 1):
                        pe.wait_ge(xnT_done, B)
                    mm = pe.matmul(bank[3][0:L, b * E:(b + 1) * E],
                                   xnT[:, c, b * L:(b + 1) * L], gw[:, c, :],
                                   start=(c == 0), stop=(c == C - 1))
                    if i == C * B - 1:
                        mm.then_inc(gated, 1)

            def hidden(k, wt, g, m, routing=False):
                n = (k * G + g) * M6 + m
                pe.wait_ge(h_mul, n + 1)
                if m == 0:
                    pe.wait_ge(ffw_lo, PIECES * k + PIECES - 2)
                    if isinstance(k, int):
                        pe.wait_ge(xn_lo_done, g + 1)
                tok = bass.ds(g * GT, GT)
                products = ([(FROM[m], P, gb, gate_mm), (MT * P + FROM[m], P, ub, up_mm)] if m != MR
                            else [(2 * MT * P, 64 + REST, gb, gate_mm)])
                for part, (first, width, to, done) in enumerate(products):
                    for c in range(C):
                        cols = slice(c * GU + first, c * GU + first + width)
                        at = 3 * (C * (2 * m + part) + c)
                        after = ((lambda n: routing_product(at + n)) if routing
                                 else lambda n: None)
                        mm = three(to[m % 2][0:width, 0:GT], w_h[wt][:, cols], w_l[wt][:, cols],
                                   xn_h[:, c, tok], xn_l[:, c, tok], c == 0, c == C - 1, after)
                    mm.then_inc(done, 1)

            def down(k, wt, g, m):
                n = (k * G + g) * M6 + m
                pe.wait_ge(h_lo_done, H0 + n + 1)
                if m == 0:
                    pe.wait_ge(y_out, Y0 + C * (k * G + g))
                if m == 4:
                    pe.wait_ge(ffw_lo, PIECES * (k + 1))
                for c in range(C):
                    cols = slice(GUW + m * D + c * P, GUW + m * D + (c + 1) * P)
                    mm = three(yb[c][:, 0:GT], w_h[wt][ROWS[m], cols], w_l[wt][ROWS[m], cols],
                               h_h[ROWS[m], m, :], h_l[ROWS[m], m, :], m == 0, m == M6 - 1)
                mm.then_inc(down_mm, 1)

            def output_rows(b):
                u = b % 2
                pe.wait_ge(acc_done, A0 + C * (G * (E - 1) + b // GB + 1))
                if b >= 2:
                    pe.wait_ge(fin, b - 1)
                for c in range(C):
                    mm = pe.transpose(rb[u][0:L, c * P:(c + 1) * P],
                                      accT[:, c, b * L:(b + 1) * L], ident[:, :])
                mm.then_inc(yt_done, 1)

            def group(k, wt, g, outputs=False, routing=False, first=False):
                for m in range(M6):
                    hidden(k, wt, g, m, routing and m < 3)
                    if first and m == 0:
                        project_out(B - 1, [(xnT_done, B - 1)])
                    if 1 <= m < M6 - 2:
                        down(k, wt, g, m - 1)
                    if outputs:
                        output_rows(2 * m)
                        output_rows(2 * m + 1)
                for m in range(M6 - 3, M6):
                    down(k, wt, g, m)

            def expert(k, wt):
                with pe.Fori(0, G) as g:
                    group(k, wt, g)

            for g in range(G // 2):
                group(0, 0, g, first=(g == 0))
            turn_ffn(B - 1, [])
            pe.wait_ge(gw_in, 16)
            group(0, 0, G // 2, routing=True)
            group(0, 0, G // 2 + 1)
            pe.wait_ge(route, ROUTED)
            pe.transpose(bM[0:E * B, 0:L], comb[:, :, :].rearrange("l e b -> l (e b)"),
                         ident[0:L, 0:L]).then_inc(comb_t, 1)
            for k in range(1, E):
                expert(k, k % 2)

            with pe.Fori(0, G - 1) as g:
                group(E, 0, g)
            group(E, 0, G - 1, True)
            for b in range(B - GB, B):
                output_rows(b)

        @block.scalar
        def _(act):
            def split_w(dst, src, loaded, at_least, done):
                act.wait_ge(loaded, at_least)
                act.activation(dst, src, ACT.Copy).then_inc(done, 1)

            def values_in(t, c):
                act.wait_ge(kvt_done, 2 * t + c + 1)
                if not (isinstance(t, int) and t == 0):
                    act.wait_ge(kv_hi_done, t)
                    act.wait_ge(kv_lo_done, t)
                    act.wait_ge(xq_done, t)
                act.activation(val[:, c, 0:S], bM[:, 0:S], ACT.Identity,
                               bias=lnw[:, 1, c:c + 1], scale=lnw[:, 0, c:c + 1])
                act.activation(val[:, c, S:SK], bM[:, S:SK], ACT.Identity,
                               bias=lnw[:, 3, c:c + 1], scale=lnw[:, 2, c:c + 1]
                               ).then_inc(val_done, 1)

            def keys_hi(t, j):
                act.wait_ge(kproj, PAIRS * t + j + 1)
                for u in range(2):
                    act.activation(keys[HEAD[u], j, u, :], key_bank(t, j)[HEAD[u], 0:KW], ACT.Copy
                                   ).then_inc(k_hi_done, 1)

            def values_out(t, i, half):
                act.wait_ge(vproj, PAIRS * t + 2 * i + half + 1)
                if not (isinstance(t, int) and t == 0):
                    act.wait_ge(pv_done, V0 + PAIRS * (t - 1) + 2 * i + 2)
                src = value_bank(t, 2 * i + half)
                act.activation(v[:, 2 * half:2 * half + 2, 2 * P * i:2 * P * (i + 1)],
                               src[0:KR, :].rearrange("p (s n) -> p s n", s=2), ACT.Copy
                               ).then_inc(v_out, 1)

            def queries_hi(t, half):
                act.wait_ge(qproj, 2 * t + half + 1)
                js = slice(4 * half, 4 * half + 4)
                for u in range(2):
                    i = act.activation(q_h[HEAD[u], js, u, :],
                                       bM[HEAD[u], 0:4 * L].rearrange("p (j l) -> p j l", j=4),
                                       ACT.Copy, scale=DH ** -0.5)
                i.then_inc(q_hi_done, 1)

            def queries_dup(t, half):
                js = slice(4 * half, 4 * half + 4)
                act.wait_ge(q_hi_done, 2 * t + half + 1)
                for u in range(2):
                    i = act.activation(q_h[HEAD[1 - u], js, u, :], SPLIT(q_h[HEAD[u], js, u, :]),
                                       ACT.Copy)
                i.then_inc(q_dup_done, 1)

            def turned_copy(b, j):
                act.wait_ge(turned, T0 + H * b + 2 * j + 1)
                act.wait_ge(pv_done, PAIRS * b + j + 1)
                act.activation(probT[:, 2 * j % 4, :, :],
                               bT[0][0:KR, 0:KT * L].rearrange("p (s l) -> p s l", s=KT), ACT.Copy
                               ).then_inc(turned_out[0], 1)

            def exps(b, j, copy=False):
                for u in range(2):
                    if copy and u == 1:
                        turned_copy(b, j - 1)
                    h = 2 * j + u
                    bS = score_banks(b, j)
                    act.wait_ge(maxed, H * b + h + 1)
                    act.wait_ge(turned, H * b + h)
                    act.activation(prob[:, h % 4, 0:SK], bS[u][0:L, 0:SK], ACT.Exp,
                                   bias=nmax[:, h:h + 1], accum_out=rsum[:, h:h + 1]
                                   ).then_inc(exped, 1)

            def heads_hi(b, half):
                act.wait_ge(pv_done, V0 + PAIRS * b + 4 * half + 4)
                act.wait_ge(wo_done, W0 + b)
                act.activation(o_h[:, 4 * half:4 * half + 4, :],
                               heads_bank(b, half)[:, 0:4 * L].rearrange(
                                   "p (j l) -> p j l", j=4), ACT.Copy
                               ).then_inc(o_hi_done, 1)

            def residual_out(b):
                act.wait_ge(ft_done, F0 + b + 1)
                act.activation(xnT[:, :, bass.ds(b * L, L)],
                               bM[:, 0:C * L].rearrange("p (c l) -> p c l", c=C), ACT.Copy
                               ).then_inc(xnT_done, 1)

            def weights_hi(wt, parts):
                for n, cols in parts:
                    i = act.activation(w_h[wt][n, cols], raw[n, cols], ACT.Copy)
                i.then_inc(ffw_hi, 1)

            def batch(b, before, next1, next2):
                for j in range(PAIRS):
                    if j > 0:
                        exps(b, j, True)
                    if before and j == 5:
                        residual_out(b - 1)
                    if isinstance(b, int) and b == 0 and j in (1, 2):
                        split_w(wo_h[:, HP * (j - 1):HP * j, :], wo_raw(j - 1), wo_in, 16, wo_hi)
                    if not next1 and 1 <= j <= PIECES:
                        if j == 1:
                            act.wait_ge(ffw_in, 64)
                            act.wait_ge(vproj, PAIRS * B)
                            act.wait_ge(qproj, 2 * B)
                        weights_hi(0, piece(j - 1) if j < PIECES - 1 else LAST[j - PIECES + 1])
                    if next1:
                        keys_hi(b + 1, j)
                        if j >= 2:
                            values_out(b + 1, (j - 2) // 2, j % 2)
                        if j == 3:
                            queries_hi(b + 1, 0)
                        if j == 4:
                            queries_dup(b + 1, 0)
                    if j == (4 if next1 else 5):
                        heads_hi(b, 0)
                    if next2 and j >= 5 and j < 7:
                        values_in(b + 2, j - 5)
                if next1:
                    queries_hi(b + 1, 1)
                turned_copy(b, PAIRS - 1)
                if next1:
                    queries_dup(b + 1, 1)
                heads_hi(b, 1)
                if next1:
                    values_out(b + 1, 3, 0)
                    values_out(b + 1, 3, 1)
                    exps(b + 1, 0)

            act.wait_ge(small_in, 48)
            act.wait_ge(const_set, 4)
            act.activation(tgate[:, :], gates[:, :], ACT.Tanh).then_inc(tanh_done, 1)
            for c in range(C):
                split_w(wkv_h[:, c, 0:INNER], raw[:, c * INNER:(c + 1) * INNER],
                        wk_in, 16 * C, wk_hi)
            values_in(0, 0)
            values_in(0, 1)
            for c in range(C):
                split_w(wkv_h[:, c, INNER:2 * INNER], raw[:, (C + c) * INNER:(C + c + 1) * INNER],
                        wv_in, 16 * C, wv_hi)
            queries_hi(0, 0)
            for j in range(PAIRS):
                keys_hi(0, j)
                if j == 3:
                    queries_dup(0, 0)
            queries_hi(0, 1)
            for i in range(PAIRS // 2):
                values_out(0, i, 0)
                if i == 1:
                    exps(0, 0)
                if i == 3:
                    queries_dup(0, 1)
                values_out(0, i, 1)
                if i in (1, 2):
                    values_in(1, i - 1)
            batch(0, False, True, True)
            with act.Fori(1, B - 2) as b:
                batch(b, True, True, True)
            batch(B - 2, True, True, False)
            batch(B - 1, True, False, False)

            def silu(m):
                units = ROWS[m] if m != MR else slice(0, REST)
                act.activation(sl[ROWS[m], m % 2, :], gb[m % 2][units, 0:GT], ACT.Silu
                               ).then_inc(silu_done, 1)

            def group(k, wt, g, routing=False):
                for m in range(M6):
                    if routing and m == 4:
                        act.wait_ge(route, 2)
                        act.activation(ex[:, :, :], lg[:, :, :], ACT.Exp).then_inc(route_exp, 1)
                    n = (k * G + g) * M6 + m
                    act.wait_ge(gate_mm, n + 1)
                    act.wait_ge(h_mul, n + 1)
                    silu(m)
                    if m == 4:
                        act.wait_ge(ffw_in, 64 * (k + 2))
                        act.wait_ge(down_mm, D0 + M6 * G * k)
                        weights_hi(1 - wt, piece(g))
                if k == 0:
                    act.wait_ge(down_mm, D0 + (k * G + g + 1) * M6)
                    for c in range(C):
                        act.activation(accT[:, c, bass.ds(g * GT, GT)], yb[c][:, 0:GT],
                                       ACT.Copy).then_inc(y_out, 1)

            def expert(k, wt):
                with act.Fori(0, G) as g:
                    group(k, wt, g)
                for parts in LAST:
                    weights_hi(1 - wt, parts)

            def last_expert(k):
                with act.Fori(0, G) as g:
                    for m in range(M6):
                        n = (k * G + g) * M6 + m
                        act.wait_ge(gate_mm, n + 1)
                        act.wait_ge(h_mul, n + 1)
                        silu(m)

            act.wait_ge(x1_done, X0 + B)
            with act.Fori(0, G // 2) as g:
                group(0, 0, g)
            residual_out(B - 1)
            group(0, 0, G // 2, True)
            for g in range(G // 2 + 1, G):
                group(0, 0, g)
            for parts in LAST:
                weights_hi(1, parts)
            for k in range(1, E):
                expert(k, k % 2)
            last_expert(E)

        @block.vector
        def _(dve):
            TILES = [(L, CT)] + [(SR, r) for r in range(CT)]

            def row_stats(t, part=(0, 1)):
                xt = x1[:, bass.ds(t, 1), :].rearrange("p a d -> p (a d)")
                if 0 in part:
                    dve.wait_ge(ctx_loaded, 16 * (t + 1))
                for n, r in [t for i in part for t in TILES[2 * i:2 * i + 2]]:
                    i = dve.bn_stats(st[0:n, r, :], ctx_raw[:, r, :] if r < CT else xt)
                if 1 not in part:
                    return
                i.then_inc(stats, 1)
                dve.wait_ge(stats, t + 1)
                plain(dve)
                for n, r in TILES:
                    i = dve.bn_aggr(mv[0:n, r, :], st[0:n, r, :])
                i.then_inc(aggr, 1)
                dve.wait_ge(aggr, t + 1)
                dve.tensor_scalar(ve[:, 0:CT], mv[:, 0:CT, 1], EPS, None, ALU.add)
                dve.tensor_scalar(ve[0:L, CT:CT + 1], mv[0:L, CT, 1:2], EPS, None, ALU.add
                                  ).then_inc(var_eps, 1)

            def row_norm(t, part):
                xt = x1[:, bass.ds(t, 1), :].rearrange("p a d -> p (a d)")
                if part == 0:
                    dve.wait_ge(rstd_done, t + 1)
                    if not (isinstance(t, int) and t == 0):
                        dve.wait_ge(kvt_done, 2 * t)
                for n, r in TILES[2 * part:2 * part + 2]:
                    dve.tensor_scalar(rows[0:n, r, :], ctx_raw[:, r, :] if r < CT else xt,
                                      mv[0:n, r, 0:1], rstd[0:n, r:r + 1],
                                      ALU.subtract, ALU.mult
                                      ).then_inc(lat_done if r == CT else ctx_norm, 1)
                if part == 1:
                    return
                dve.wait_ge(lat_done, t + 1)
                dve.bn_stats(lst[:, :], rows[0:L, CT, :]).then_inc(lstats, 1)
                dve.wait_ge(lstats, t + 1)
                plain(dve)
                dve.bn_aggr(lmv[:, :], lst[:, :]).then_inc(laggr, 1)
                dve.wait_ge(laggr, t + 1)
                dve.tensor_scalar(lve[:, :], lmv[:, 1:2], EPS, None, ALU.add
                                  ).then_inc(lvar_eps, 1)

            def latent_norm(t):
                dve.wait_ge(lrstd_done, t + 1)
                dve.tensor_scalar(rows[0:L, CT, :], rows[0:L, CT, :], lmv[:, 0:1], lrstd[:, 0:1],
                                  ALU.subtract, ALU.mult).then_inc(rows_done, 1)

            def split_lo(dst, full, hi, waits, done):
                for s, at_least in waits:
                    dve.wait_ge(s, at_least)
                dve.tensor_tensor(dst, full, SPLIT(hi), ALU.subtract).then_inc(done, 1)

            def values_in_hi(t):
                dve.wait_ge(val_done, 2 * t + 2)
                if not (isinstance(t, int) and t == 0):
                    dve.wait_ge(vproj, PAIRS * t)
                dve.tensor_copy(kv_h[:, :, :], val[:, :, :]).then_inc(kv_hi_done, 1)

            def values_in_lo(t):
                dve.wait_ge(kv_hi_done, t + 1)
                dve.tensor_tensor(kv_l[:, :, :], val[:, :, :], SPLIT(kv_h[:, :, :]),
                                  ALU.subtract).then_inc(kv_lo_done, 1)

            def keys_lo(t, j):
                for u in range(2):
                    dve.wait_ge(k_hi_done, H * t + 2 * j + u + 1)
                    i = dve.tensor_tensor(keys[HEAD[1 - u], j, u, :],
                                          key_bank(t, j)[HEAD[u], 0:KW],
                                          SPLIT(keys[HEAD[u], j, u, :]), ALU.subtract)
                i.then_inc(k_lo_done, 1)

            def queries_lo(t, half):
                dve.wait_ge(q_hi_done, 2 * t + half + 1)
                js = slice(4 * half, 4 * half + 4)
                for u in range(2):
                    i = dve.scalar_tensor_tensor(
                        q_l[HEAD[u], js, :],
                        bM[HEAD[u], 0:4 * L].rearrange("p (j l) -> p j l", j=4), DH ** -0.5,
                        SPLIT(q_h[HEAD[u], js, u, :]), ALU.mult, ALU.subtract)
                i.then_inc(q_lo_done, 1)

            def maxima(b, j):
                for u in range(2):
                    h = 2 * j + u
                    bS = score_banks(b, j)
                    dve.wait_ge(scored, H * b + h + 1)
                    dve.tensor_reduce(nmax[:, h:h + 1], bS[u][0:L, 0:SK], AX.X, ALU.max,
                                      negate=True).then_inc(maxed, 1)

            def invert(b, h):
                dve.wait_ge(exped, S0 + H * b + h + 1)
                dve.reciprocal(rinv[:, h:h + 1], rsum[:, h:h + 1]).then_inc(inverted, 1)

            def turned_copy(b, j):
                dve.wait_ge(turned, T0 + H * b + 2 * j + 2)
                dve.wait_ge(pv_done, PAIRS * b + j + 1)
                dve.tensor_copy(probT[:, (2 * j + 1) % 4, :, :],
                                bT[1][0:KR, 0:KT * L].rearrange("p (s l) -> p s l", s=KT)
                                ).then_inc(turned_out[1], 1)

            def heads_lo(b, half):
                js = slice(4 * half, 4 * half + 4)
                split_lo(o_l[:, js, :],
                         heads_bank(b, half)[:, 0:4 * L].rearrange("p (j l) -> p j l", j=4),
                         o_h[:, js, :], [(o_hi_done, 2 * b + half + 1)], o_lo_done)

            def rows_of(b):
                return x1[:, bass.ds(b, 1), :].rearrange("p a d -> p (a d)")

            def residual(b):
                dve.wait_ge(wo_done, W0 + b + 1)
                dve.scalar_tensor_tensor(rows_of(b), bM[0:L, 0:D], tgate[0:L, 0:1], rows_of(b),
                                         ALU.mult, ALU.add).then_inc(x1_done, 1)

            def residual_stats(b):
                dve.wait_ge(x1_done, X0 + b + 1)
                dve.bn_stats(fst[:, :], rows_of(b)).then_inc(fstats, 1)
                dve.wait_ge(fstats, b + 1)
                plain(dve)
                dve.bn_aggr(fmv[:, :], fst[:, :]).then_inc(faggr, 1)
                dve.wait_ge(faggr, b + 1)
                dve.tensor_scalar(fve[:, :], fmv[:, 1:2], EPS, None, ALU.add
                                  ).then_inc(fve_done, 1)

            def residual_norm(b):
                dve.wait_ge(frstd_done, b + 1)
                dve.wait_ge(ft_done, F0 + b)
                dve.tensor_scalar(frow[:, :], rows_of(b), fmv[:, 0:1], frstd[:, 0:1],
                                  ALU.subtract, ALU.mult).then_inc(frow_done, 1)

            def tokens_hi(g):
                tok = slice(g * GT, (g + 1) * GT)
                dve.tensor_copy(xn_h[:, :, tok], xnT[:, :, tok]).then_inc(xn_hi_done, 1)

            def weights_lo(count, parts):
                dve.wait_ge(ffw_hi, count)
                for n, cols in parts:
                    i = dve.tensor_tensor(w_l[0][n, cols], raw[n, cols],
                                          SPLIT(w_h[0][n, cols]), ALU.subtract)
                i.then_inc(ffw_lo, 1)

            def batch(b, before, next1, next2):
                for j in range(PAIRS):
                    if j > 0:
                        maxima(b, j)
                        turned_copy(b, j - 1)
                    if before and j == 0:
                        residual_stats(b - 1)
                    if before and j == 1:
                        residual_norm(b - 1)
                    if next2:
                        if j in (1, 2):
                            row_stats(b + 2, (j - 1,))
                        if j in (3, 5):
                            row_norm(b + 2, (j - 3) // 2)
                        if j == 5:
                            latent_norm(b + 2)
                    if next1 and j == 4:
                        queries_lo(b + 1, 0)
                    if j > 0:
                        invert(b, 2 * j)
                        invert(b, 2 * j + 1)
                    if not next1 and 2 <= j < PIECES:
                        weights_lo(j - 1, piece(j - 2))
                    if next1:
                        keys_lo(b + 1, j)
                    if j == (4 if next1 else 5):
                        heads_lo(b, 0)
                if next1:
                    queries_lo(b + 1, 1)
                if not next1:
                    dve.wait_ge(scored, H * B)
                    dve.wait_ge(xnT_done, GB)
                    tokens_hi(0)
                turned_copy(b, PAIRS - 1)
                heads_lo(b, 1)
                if not next1:
                    for n in range(2):
                        weights_lo(PIECES - 1 + n, LAST[n])
                if next2:
                    values_in_hi(b + 2)
                if next1:
                    maxima(b + 1, 0)
                    invert(b + 1, 0)
                    invert(b + 1, 1)
                residual(b)

            dve.wait_ge(x_in, 16)
            row_stats(0)
            row_norm(0, 0)
            row_norm(0, 1)
            latent_norm(0)
            for c in range(C):
                split_lo(wkv_l[:, c, 0:INNER], raw[:, c * INNER:(c + 1) * INNER],
                         wkv_h[:, c, 0:INNER], [(wk_hi, c + 1)], wk_lo)
            values_in_hi(0)
            values_in_lo(0)
            row_stats(1)
            queries_lo(0, 0)
            for j in range(PAIRS):
                keys_lo(0, j)
            queries_lo(0, 1)
            row_norm(1, 0)
            row_norm(1, 1)
            maxima(0, 0)
            latent_norm(1)
            invert(0, 0)
            invert(0, 1)
            values_in_hi(1)
            values_in_lo(1)
            dve.wait_ge(x_rest_in, 16)
            dve.wait_ge(tanh_done, 1)
            batch(0, False, True, True)
            with dve.Fori(1, B - 2) as b:
                batch(b, True, True, True)
            batch(B - 2, True, True, False)
            batch(B - 1, True, False, False)

            def over_e(ap):
                return ap.unsqueeze(2).broadcast_to((L, B, E))

            scores = bank[3][0:L, 0:B * E].rearrange("p (b e) -> p b e", e=E)

            def before_each():
                for f in range(E):
                    def score_f(n):
                        return sc[:, :, f:f + 1].broadcast_to((L, B, n))
                    i = dve.tensor_tensor(beat[:, f, :, 0:f + 1], score_f(f + 1),
                                          sc[:, :, 0:f + 1], ALU.is_gt)
                    if f < E - 1:
                        i = dve.tensor_tensor(beat[:, f, :, f + 1:E], score_f(E - 1 - f),
                                              sc[:, :, f + 1:E], ALU.is_ge)
                return i

            def route_step(n):
                if n == 0:
                    dve.wait_ge(gated, 1)
                    i = dve.tensor_reduce(lmax[:, :], scores, AX.X, ALU.max)
                else:
                    dve.wait_ge(route, n)
                if n == 1:
                    i = dve.tensor_tensor(lg[:, :, :], scores, over_e(lmax[:, :]), ALU.subtract)
                if n == 2:
                    dve.wait_ge(route_exp, 1)
                    i = dve.tensor_reduce(esum[:, :], ex[:, :, :], AX.X, ALU.add)
                if n == 3:
                    i = dve.reciprocal(wsum[:, :], esum[:, :])
                if n == 4:
                    i = dve.tensor_tensor(sc[:, :, :], ex[:, :, :], over_e(wsum[:, :]), ALU.mult)
                if n == 5:
                    i = before_each()
                if n == 6:
                    i = dve.tensor_reduce(rank[:, :, :],
                                          beat[:, :, :, :].rearrange("p f b e -> p b e f"),
                                          AX.X, ALU.add)
                if n == 7:
                    i = dve.scalar_tensor_tensor(wsel[:, :, :], rank[:, :, :], 1.5, sc[:, :, :],
                                                 ALU.is_lt, ALU.mult)
                if n == 8:
                    i = dve.tensor_reduce(esum[:, :], wsel[:, :, :], AX.X, ALU.add)
                if n == 9:
                    i = dve.tensor_scalar(esum[:, :], esum[:, :], 1e-20, None, ALU.add)
                if n == 10:
                    i = dve.reciprocal(wsum[:, :], esum[:, :])
                if n == 11:
                    i = dve.tensor_tensor(comb[:, :, :].rearrange("p e b -> p b e"),
                                          wsel[:, :, :], over_e(wsum[:, :]), ALU.mult)
                i.then_inc(route, 1)

            def output(b):
                dve.wait_ge(yt_done, b + 1)
                dve.scalar_tensor_tensor(rows_of(b), rb[b % 2][0:L, 0:D], tgate[0:L, 1:2],
                                         rows_of(b), ALU.mult, ALU.add).then_inc(fin, 1)

            def group(k, wt, g, after=lambda m: None):
                for m in range(M6):
                    n = (k * G + g) * M6 + m
                    dve.wait_ge(silu_done, n + 1)
                    if m != MR:
                        dve.wait_ge(up_mm, (k * G + g) * MT + min(m + 1, MT))
                    dve.wait_ge(h_lo_done, n + 1)
                    up = ub[m % 2] if m != MR else gb[m % 2]
                    dve.tensor_tensor(hf[ROWS[m], m % 2, :], up[ROWS[m], 0:GT],
                                      sl[ROWS[m], m % 2, :], ALU.mult).then_inc(h_mul, 1)
                    dve.wait_ge(h_mul, H0 + n + 1)
                    dve.wait_ge(down_mm, D0 + M6 * (k * G + g))
                    dve.tensor_copy(h_h[ROWS[m], m, :], hf[ROWS[m], m % 2, :]
                                    ).then_inc(h_hi_done, 1)
                    split_lo(h_l[ROWS[m], m, :], hf[ROWS[m], m % 2, :], h_h[ROWS[m], m, :],
                             [(h_hi_done, n + 1)], h_lo_done)
                    after(m)

            def weighted(k, wt, g, turn):
                dve.wait_ge(cb_in[wt], 16 * turn)
                dve.wait_ge(down_mm, D0 + (k * G + g + 1) * M6)
                dve.wait_ge(acc_done, A0 + C * ((k - 1) * G + g))
                for c in range(C):
                    dve.tensor_tensor(ytmp[:, c, :], yb[c][:, 0:GT],
                                      cb[wt][:, bass.ds(g * GT, GT)], ALU.mult
                                      ).then_inc(y_out, 1)

            def expert(k, wt, turn):
                with dve.Fori(0, G) as g:
                    group(k, wt, g)
                    weighted(k, wt, g, turn)

            def rows_and_tokens(m):
                if m == 0:
                    residual_stats(B - 1)
                if m == 2:
                    residual_norm(B - 1)
                if m in (1, 3):
                    g = (m + 1) // 2
                    dve.wait_ge(xnT_done, (g + 1) * GB)
                    tokens_hi(g)

            def routing(m, first):
                for n in range(first + 2 * m, first + 2 * m + 2):
                    if 0 <= n < ROUTED:
                        route_step(n)

            def outputs(m):
                output(2 * m)
                output(2 * m + 1)

            group(0, 0, 0, rows_and_tokens)
            group(0, 0, 1)
            dve.wait_ge(xnT_done, B)
            tokens_hi(G - 1)
            group(0, 0, 2, lambda m: routing(m, -6) if m == 3 else None)
            group(0, 0, 3, lambda m: routing(m, 2))
            dve.wait_ge(comb_t, 1)
            dve.tensor_copy(combT[:, :], bM[0:E * B, 0:L]).then_inc(comb_c, 1)
            for k in range(1, E):
                expert(k, k % 2, (k + 1) // 2)
            with dve.Fori(0, G - 1) as g:
                group(E, 0, g)
                weighted(E, 0, g, E // 2)
            group(E, 0, G - 1, outputs)
            weighted(E, 0, G - 1, E // 2)
            dve.wait_ge(y_out, Y0 + C * G * E1)
            last = accT[:, 1, (G - 1) * GT:N]
            dve.tensor_tensor(last, last, ytmp[:, 1, :], ALU.add).then_inc(acc_done, 1)
            for b in range(B - GB, B):
                output(b)

        @block.gpsimd
        def _(pool):
            pool.memset(ident[:, :], 0.0).then_inc(ident0, 1)
            pool.memset(neghalf[:, :], -0.5).then_inc(const_set, 1)
            pool.memset(val[:, :, SK:KW], 0.0).then_inc(const_set, 1)
            pool.memset(prob[:, :, SK:KW], 0.0).then_inc(const_set, 1)
            pool.wait_ge(ident0, 1)
            pool.affine_select(out=ident[:, :], in_=ident[:, :], compare_op=ALU.not_equal,
                               fill=1.0, base=0, pattern=[[-1, P]], channel_multiplier=1
                               ).then_inc(const_set, 1)
            for s, start in ((exped, S0), (turned, T0), (pv_done, V0),
                             (turned_out[0], C0), (turned_out[1], C0),
                             (o_lo_done, O0), (x1_done, X0), (wo_done, W0), (ft_done, F0),
                             (h_mul, H0), (h_lo_done, H0),
                             (down_mm, D0), (y_out, Y0), (acc_done, A0)):
                pool.sem_inc(s, start)
            pool.wait_ge(const_set, 4)

            def power(dst, src, cols):
                return pool.tensor_tensor(dst, src, cols, ALU.pow)

            def row_rstd(t):
                pool.wait_ge(var_eps, t + 1)
                power(rstd[:, 0:CT], ve[:, 0:CT], neghalf[0:SR, 0:CT])
                power(rstd[0:L, CT:CT + 1], ve[0:L, CT:CT + 1], neghalf[0:L, 0:1]
                      ).then_inc(rstd_done, 1)

            def latent_rstd(t):
                pool.wait_ge(lvar_eps, t + 1)
                power(lrstd[:, :], lve[:, :], neghalf[0:L, 0:1]).then_inc(lrstd_done, 1)

            def normalise(b, j):
                for u in range(2):
                    h = 2 * j + u
                    pool.wait_ge(inverted, H * b + h + 1)
                    plain(pool)
                    pool.tensor_scalar(prob[:, h % 4, 0:SK], prob[:, h % 4, 0:SK],
                                       rinv[:, h:h + 1], 1.0, ALU.mult, ALU.mult
                                       ).then_inc(normed, 1)

            def queries_in(t):
                pool.wait_ge(val_done, 2 * t + 2)
                if not (isinstance(t, int) and t == 0):
                    pool.wait_ge(qproj, 2 * t)
                    plain(pool)
                pool.tensor_copy(xq[:, :, :], val[:, :, S:SK]).then_inc(xq_done, 1)

            def values_in_lo(t):
                pool.wait_ge(kv_hi_done, t + 1)
                pool.tensor_tensor(kv_l[:, :, :], val[:, :, :], SPLIT(kv_h[:, :, :]),
                                   ALU.subtract).then_inc(kv_lo_done, 1)

            def residual_rstd(b):
                pool.wait_ge(fve_done, b + 1)
                power(frstd[:, :], fve[:, :], neghalf[0:L, 0:1]).then_inc(frstd_done, 1)

            def weights_lo(wt, count, parts):
                pool.wait_ge(ffw_hi, count)
                pool.wait_ge(ffw_lo, count - 1)
                for n, cols in parts:
                    i = pool.tensor_tensor(w_l[wt][n, cols], raw[n, cols],
                                           SPLIT(w_h[wt][n, cols]), ALU.subtract)
                i.then_inc(ffw_lo, 1)

            def tokens_lo(g):
                tok = slice(g * GT, (g + 1) * GT)
                pool.wait_ge(xn_hi_done, g + 1)
                pool.tensor_tensor(xn_l[:, :, tok], xnT[:, :, tok], SPLIT(xn_h[:, :, tok]),
                                   ALU.subtract).then_inc(xn_lo_done, 1)

            def project_out_lo(n):
                pool.wait_ge(wo_hi, n + 1)
                js = slice(HP * n, HP * (n + 1))
                pool.tensor_tensor(wo_l[:, js, :], wo_raw(n), SPLIT(wo_h[:, js, :]), ALU.subtract
                                   ).then_inc(wo_lo, 1)

            def batch(b, before, next1, next2):
                for j in range(PAIRS):
                    if before and j == 1:
                        residual_rstd(b - 1)
                    if j > 0:
                        normalise(b, j)
                    if isinstance(b, int) and b == 0 and j in (2, 3):
                        project_out_lo(j - 2)
                    if next2 and j == 2:
                        row_rstd(b + 2)
                    if next2 and j == 3:
                        latent_rstd(b + 2)
                if next2:
                    values_in_lo(b + 2)
                    queries_in(b + 2)
                if next1:
                    normalise(b + 1, 0)

            row_rstd(0)
            latent_rstd(0)
            queries_in(0)
            row_rstd(1)
            for c in range(C):
                pool.wait_ge(wv_hi, c + 1)
                pool.tensor_tensor(wkv_l[:, c, INNER:2 * INNER],
                                   raw[:, (C + c) * INNER:(C + c + 1) * INNER],
                                   SPLIT(wkv_h[:, c, INNER:2 * INNER]), ALU.subtract
                                   ).then_inc(wv_lo, 1)
            latent_rstd(1)
            normalise(0, 0)
            queries_in(1)
            batch(0, False, True, True)
            with pool.Fori(1, B - 2) as b:
                batch(b, True, True, True)
            batch(B - 2, True, True, False)
            batch(B - 1, True, False, False)

            tokens_lo(0)
            residual_rstd(B - 1)
            for g in range(1, G - 1):
                tokens_lo(g)

            def added(k, g, chunks=C):
                for c in range(chunks):
                    acc = accT[:, c, bass.ds(g * GT, GT)]
                    pool.wait_ge(y_out, Y0 + C * (k * G + g) + c + 1)
                    pool.tensor_tensor(acc, acc, ytmp[:, c, :], ALU.add).then_inc(acc_done, 1)

            def expert(k, wt):
                with pool.Fori(0, G) as g:
                    weights_lo(1 - wt, PIECES * (k + 1) + g + 1, piece(g))
                    added(k, g)
                for n in range(2):
                    weights_lo(1 - wt, PIECES * (k + 2) - 1 + n, LAST[n])

            with pool.Fori(0, G - 1) as g:
                weights_lo(1, PIECES + g + 1, piece(g))
            tokens_lo(G - 1)
            weights_lo(1, PIECES + G, piece(G - 1))
            for n in range(2):
                weights_lo(1, 2 * PIECES - 1 + n, LAST[n])
            for k in range(1, E):
                expert(k, k % 2)
            with pool.Fori(0, G - 1) as g:
                added(E, g)
            added(E, G - 1, 1)


def kernel(x, ctx_1024, g_xattn, g_ffn, L0_xattn_Wq, L0_xattn_Wkv, L0_xattn_Wo, L0_xattn_ln1_w,
           L0_xattn_ln1_b, L0_xattn_ln2_w, L0_xattn_ln2_b, L0_ffn_gate_w, L0_ffn_eg, L0_ffn_eu,
           L0_ffn_ed, L0_ffn_sg, L0_ffn_su, L0_ffn_sd):
    import numpy as np
    import concourse.bacc as bacc
    from concourse.bass_utils import run_bass_kernel_spmd

    def experts(shared, routed):
        both = np.concatenate([np.asarray(shared)[None], np.asarray(routed)])
        return both.transpose(0, 2, 1)

    gateT, upT = experts(L0_ffn_sg, L0_ffn_eg), experts(L0_ffn_su, L0_ffn_eu)
    full = gateT.shape[2] // P * P
    pad = np.zeros(gateT.shape[:2] + (64 - gateT.shape[2] % P,), gateT.dtype)
    gate_upT = np.concatenate([gateT[:, :, :full], upT[:, :, :full], gateT[:, :, full:], pad,
                               upT[:, :, full:]], axis=2)

    ln_wb = np.stack([np.asarray(a).reshape(-1, P) for a in (
        L0_xattn_ln1_w, L0_xattn_ln1_b, L0_xattn_ln2_w, L0_xattn_ln2_b)]).transpose(2, 0, 1)

    ins = [("x", x), ("ctx", ctx_1024), ("g_xattn", g_xattn), ("g_ffn", g_ffn),
           ("wq", L0_xattn_Wq), ("wkv", L0_xattn_Wkv), ("wo", L0_xattn_Wo),
           ("ln_wb", ln_wb),
           ("gate_wT", np.asarray(L0_ffn_gate_w).T),
           ("gate_upT", gate_upT),
           ("downT", experts(L0_ffn_sd, L0_ffn_ed))]
    nc = bacc.Bacc("TRN2", target_bir_lowering=False, num_devices=1)
    arrays, aps = {}, []
    for name, a in ins:
        a = np.ascontiguousarray(a)
        arrays[f"in_{name}"] = a
        aps.append(nc.dram_tensor(f"in_{name}", a.shape, mybir.dt.from_np(a.dtype),
                                  kind="ExternalInput").ap())
    shape = np.asarray(x).shape
    out = nc.dram_tensor("out_x", shape, F32, kind="ExternalOutput").ap()
    flamingo_block(nc, *aps, out)
    r = run_bass_kernel_spmd(nc, [arrays], core_ids=[0])
    return r.results[0]["out_x"]
```
